# Optimizing a Trainium2 kernel written in Bass

```python
import numpy as np
import jax
import jax.numpy as jnp

def _softmax(x, axis=-1):
    return jax.nn.softmax(x, axis=axis)

def _gelu(x):
    return jax.nn.gelu(x, approximate=True)

def _silu(x):
    return jax.nn.silu(x)

def _sigmoid(x):
    return jax.nn.sigmoid(x)

def _layernorm(x, axis=-1, eps=1e-05):
    m = jnp.mean(x, axis=axis, keepdims=True)
    v = jnp.var(x, axis=axis, keepdims=True)
    return (x - m) / jnp.sqrt(v + eps)

def _scatter_add(tgt, idx, src, axis=0):
    return tgt.at[idx].add(src)

def _segment_sum(src, seg, n):
    return jax.ops.segment_sum(src, seg, n)
kernel_name = 'mk_xattn_ffn_d1_seqx_r8_17efa5'

def setup_inputs(seed: int=0):
    np.random.seed(seed)
    _w = jnp.asarray

    def _rec_inputs():
        import jax
        import jax.numpy as jnp
        _rk = jax.random.key(seed)
        x = 7.22e-05 + 1 * jax.random.normal(jax.random.fold_in(_rk, 1), (32, 64, 512), jnp.float32)
        _lenS = 64 - jax.random.randint(jax.random.fold_in(_rk, 7), (32,), 0, max(1, 64 // 4) + 1, jnp.int32)
        _lenS2 = 64 - jax.random.randint(jax.random.fold_in(_rk, 8), (32,), 0, max(1, 64 // 4) + 1, jnp.int32)
        _ctx_4096P = jax.random.normal(jax.random.fold_in(_rk, 11), (32, 16, 512), jnp.float32)
        _ctx_4096c = jax.random.dirichlet(jax.random.fold_in(_rk, 511), 0.3 * jnp.ones((16,), jnp.float32), (32, 64))
        _ctx_4096t = jnp.einsum('bsk,bkd->bsd', _ctx_4096c, _ctx_4096P)
        _ctx_4096t = _ctx_4096t * jax.lax.rsqrt(jnp.mean(jnp.square(_ctx_4096t)) + 1e-12) * 0.953939
        ctx_4096 = 4.13588e-05 + 0.999923 * (_ctx_4096t + 0.3 * jax.random.normal(jax.random.fold_in(_rk, 611), (32, 64, 512), jnp.float32))
        return (x, ctx_4096)
    x, ctx_4096 = _rec_inputs()

    def _L0_xattn_setup():
        import jax, jax.numpy as jnp
        import numpy as np
        HEADS = 8
        WINDOW = 16

        def _pointwise(W, b, t):
            return jnp.einsum('oc,bct->bot', W, t) + b[None, :, None]
        key = jax.random.key(seed)
        ks = jax.random.split(key, 10)
        B, C, T = (4, 64, 512)
        s = 0.02
        return {'x': jax.random.normal(ks[0], (B, C, T), jnp.float32), 'cond': jax.random.normal(ks[1], (B, C, T), jnp.float32), 'Wq': jax.random.normal(ks[2], (C, C), jnp.float32) * s, 'bq': jnp.zeros((C,), jnp.float32), 'Wk': jax.random.normal(ks[3], (C, C), jnp.float32) * s, 'bk': jnp.zeros((C,), jnp.float32), 'Wv': jax.random.normal(ks[4], (C, C), jnp.float32) * s, 'bv': jnp.zeros((C,), jnp.float32), 'Wo': jax.random.normal(ks[5], (C, C), jnp.float32) * s, 'bo': jnp.zeros((C,), jnp.float32)}
    _L0_xattn_all = _L0_xattn_setup()
    _L0_xattn_in = {k: v for k, v in _L0_xattn_all.items() if k in ('Wq', 'bq', 'Wk', 'bk', 'Wv', 'bv', 'Wo', 'bo')}
    del _L0_xattn_all

    def _L0_ffn_setup():
        import jax, jax.numpy as jnp
        import numpy as np
        BITS = 4
        GROUP_SIZE = 128
        IN_FEATURES = 512
        OUT_FEATURES = 512
        BATCH, SEQ = (4, 256)

        def dequantize(qweight, qzeros, scales, g_idx, bits=BITS):
            pack = 32 // bits
            maxq = (1 << bits) - 1
            K = qweight.shape[0] * pack
            N = qweight.shape[1]
            ki = jnp.arange(K, dtype=jnp.int32)
            w = qweight[ki // pack] >> (ki % pack * bits)[:, None] & maxq
            ni = jnp.arange(N, dtype=jnp.int32)
            z = qzeros[:, ni // pack] >> (ni % pack * bits)[None, :] & maxq
            return (w - z[g_idx]).astype(scales.dtype) * scales[g_idx]
        key = jax.random.key(seed)
        k1, k2, k3, k4, k5 = jax.random.split(key, 5)
        n_groups = IN_FEATURES // GROUP_SIZE
        pack = 32 // BITS
        x = jax.random.normal(k1, (BATCH, SEQ, IN_FEATURES), dtype=jnp.float16)
        qweight = jax.random.randint(k2, (IN_FEATURES // 32 * BITS, OUT_FEATURES), 0, 2147483647, dtype=jnp.int32)
        qzeros = jax.random.randint(k3, (n_groups, OUT_FEATURES // 32 * BITS), 0, 2147483647, dtype=jnp.int32)
        scales = (jax.random.uniform(k4, (n_groups, OUT_FEATURES), dtype=jnp.float32) * 0.01 + 0.001).astype(jnp.float16)
        g_idx = jnp.arange(IN_FEATURES, dtype=jnp.int32) // GROUP_SIZE
        bias = jax.random.normal(k5, (OUT_FEATURES,), dtype=jnp.float16)
        return {'x': x, 'qweight': qweight, 'qzeros': qzeros, 'scales': scales, 'g_idx': g_idx, 'bias': bias}
    _L0_ffn_all = _L0_ffn_setup()
    _L0_ffn_in = {k: v for k, v in _L0_ffn_all.items() if k in ('qweight', 'qzeros', 'scales', 'g_idx', 'bias')}
    del _L0_ffn_all
    return {'x': x, 'ctx_4096': ctx_4096, 'L0_xattn_Wq': _L0_xattn_in['Wq'], 'L0_xattn_bq': _L0_xattn_in['bq'], 'L0_xattn_Wk': _L0_xattn_in['Wk'], 'L0_xattn_bk': _L0_xattn_in['bk'], 'L0_xattn_Wv': _L0_xattn_in['Wv'], 'L0_xattn_bv': _L0_xattn_in['bv'], 'L0_xattn_Wo': _L0_xattn_in['Wo'], 'L0_xattn_bo': _L0_xattn_in['bo'], 'L0_ffn_qweight': _L0_ffn_in['qweight'], 'L0_ffn_qzeros': _L0_ffn_in['qzeros'], 'L0_ffn_scales': _L0_ffn_in['scales'], 'L0_ffn_g_idx': _L0_ffn_in['g_idx'], 'L0_ffn_bias': _L0_ffn_in['bias']}

def reference(x, ctx_4096, L0_xattn_Wq, L0_xattn_bq, L0_xattn_Wk, L0_xattn_bk, L0_xattn_Wv, L0_xattn_bv, L0_xattn_Wo, L0_xattn_bo, L0_ffn_qweight, L0_ffn_qzeros, L0_ffn_scales, L0_ffn_g_idx, L0_ffn_bias):
    import jax
    import jax.numpy as jnp

    def _L0_xattn_ref(x, cond, Wq, bq, Wk, bk, Wv, bv, Wo, bo):
        import jax, jax.numpy as jnp
        import numpy as np
        HEADS = 8
        WINDOW = 16

        def _pointwise(W, b, t):
            return jnp.einsum('oc,bct->bot', W, t) + b[None, :, None]
        B, C, T = x.shape
        H, W = (HEADS, WINDOW)
        hd = C // H
        scale = hd ** (-0.5)
        pad_left = W // 2
        pad_right = W - pad_left - 1
        q = _pointwise(Wq, bq, x)
        k = _pointwise(Wk, bk, cond)
        v = _pointwise(Wv, bv, cond)
        k = jnp.pad(k, ((0, 0), (0, 0), (pad_left, pad_right)))
        v = jnp.pad(v, ((0, 0), (0, 0), (pad_left, pad_right)))
        idx = jnp.arange(T)[:, None] + jnp.arange(W)[None, :]
        k_win = k[:, :, idx].reshape(B, H, hd, T, W)
        v_win = v[:, :, idx].reshape(B, H, hd, T, W)
        qh = q.reshape(B, H, hd, T)
        dots = jnp.einsum('bhdt,bhdtw->bhtw', qh, k_win) * scale
        attn = jax.nn.softmax(dots, axis=-1)
        out = jnp.einsum('bhtw,bhdtw->bhdt', attn, v_win)
        out = out.reshape(B, C, T)
        return _pointwise(Wo, bo, out)

    def _L0_ffn_ref(x, qweight, qzeros, scales, g_idx, bias):
        import jax, jax.numpy as jnp
        import numpy as np
        BITS = 4
        GROUP_SIZE = 128
        IN_FEATURES = 512
        OUT_FEATURES = 512
        BATCH, SEQ = (4, 256)

        def dequantize(qweight, qzeros, scales, g_idx, bits=BITS):
            pack = 32 // bits
            maxq = (1 << bits) - 1
            K = qweight.shape[0] * pack
            N = qweight.shape[1]
            ki = jnp.arange(K, dtype=jnp.int32)
            w = qweight[ki // pack] >> (ki % pack * bits)[:, None] & maxq
            ni = jnp.arange(N, dtype=jnp.int32)
            z = qzeros[:, ni // pack] >> (ni % pack * bits)[None, :] & maxq
            return (w - z[g_idx]).astype(scales.dtype) * scales[g_idx]
        W = dequantize(qweight, qzeros, scales, g_idx)
        x2d = x.reshape(-1, x.shape[-1])
        out = jnp.matmul(x2d, W, preferred_element_type=jnp.float32)
        out = out.astype(jnp.float16).reshape(x.shape[:-1] + (W.shape[1],))
        out = out + bias
        return out.astype(x.dtype)
    x = x + _L0_xattn_ref(_layernorm(x, axis=-1), ctx_4096, L0_xattn_Wq, L0_xattn_bq, L0_xattn_Wk, L0_xattn_bk, L0_xattn_Wv, L0_xattn_bv, L0_xattn_Wo, L0_xattn_bo)
    x = x + _L0_ffn_ref(_layernorm(x, axis=-1), L0_ffn_qweight, L0_ffn_qzeros, L0_ffn_scales, L0_ffn_g_idx, L0_ffn_bias)
    return x

_drawn_inputs = setup_inputs


def setup_inputs(seed=0):
    import zlib

    import numpy as np

    out = dict(_drawn_inputs(seed))
    spreads = {'L0_xattn_bq': (0.0, 0.8),
     'L0_xattn_bk': (0.0, 2.0),
     'L0_xattn_bv': (0.0, 0.8),
     'L0_xattn_bo': (0.0, 0.302)}
    factors = {'ctx_4096': 6.214,
     'L0_xattn_Wq': 8.0,
     'L0_xattn_Wk': 8.0,
     'L0_xattn_Wv': 5.99,
     'L0_xattn_Wo': 3.916}
    for name, (base, spread) in spreads.items():
        noise = np.random.default_rng([zlib.crc32(name.encode()), seed]).standard_normal(out[name].shape)
        drawn = base * np.exp(spread * noise) if base else spread * noise
        out[name] = jnp.asarray(drawn.astype(out[name].dtype))
    for name, factor in factors.items():
        out[name] = (out[name] * factor).astype(out[name].dtype)
    return out
```

```python
from contextlib import ExitStack

import concourse.bass as bass
from concourse import mybir

F32 = mybir.dt.float32
BF16 = mybir.dt.bfloat16
F16 = mybir.dt.float16
I32 = mybir.dt.int32
ALU = mybir.AluOpType
ACT = mybir.ActivationFunctionType
AX = mybir.AxisListType

P = 128
B, C, T = 32, 64, 512
H, WIN = 8, 16
HD = C // H
PAIRS = 2
NB = 2 * PAIRS
STEPS = B // NB
QB = 16
KB = 32
NU = T // QB
LEFT = WIN // 2
TP = (NU - 1) * QB + KB
OCT = 8
NQ = NU // 4
SLOTS = 8
GROUPS, IN_F, OUT_F = 4, 512, 512
NIB = 8
KC = IN_F // P
EPS = 1e-5
MASKED = -1e30
T_LAG, AV_LAG = 4, 5
S_BANKS = 3
LEVELS = 5
LAST_ON_BANK = {0: 6, 1: 7, 2: 5}


class Step:

    def __init__(self, i, k):
        self.i, self.k = i, k
        self.par = k % 2

    def after(self, per, event=0):
        return self.i * (2 * per) + (self.k * per + event + 1)

    def before(self, per):
        return self.i * (2 * per) + self.k * per

    def shift(self, d):
        return Step(self.i, self.k + d)


def run_steps(eng, step):
    step(Step(0, 0), False, True, True)
    step(Step(0, 1), True, True, True)
    with eng.Fori(0, (STEPS - 4) // 2) as i:
        step(Step(i, 2), True, True, True)
        step(Step(i, 3), True, True, True)
    step(Step(0, STEPS - 2), True, True, True)
    step(Step(0, STEPS - 1), True, True, False)
    step(Step(0, STEPS), True, False, False)


def build(nc, x, ctx_in, wq, bq, wk, bk, wv, bv, wo, bo, qweight, qzeros, scales, g_idx, bias, out):
    x_v = x.rearrange("(n q b) c t -> n (b c) q t", q=PAIRS, b=2)
    ctx_v = ctx_in.rearrange("(n q b) c t -> n (b c) q t", q=PAIRS, b=2)
    out_v = out.rearrange("(n q b) c t -> n (b c) q t", q=PAIRS, b=2)

    with ExitStack() as es:
        def sb(name, shape, dt=F32):
            return es.enter_context(nc.sbuf_tensor(name, shape, dt))

        def ps(name):
            return es.enter_context(nc.psum_tensor(name, [P, 512], F32))

        def sem(name):
            return es.enter_context(nc.semaphore(name))

        x_sb = sb("x_sb", [P, PAIRS, T])
        c_sb = sb("c_sb", [P, PAIRS, T])
        stats = sb("stats", [P, PAIRS, 6])
        mean_var = sb("mean_var", [P, PAIRS, 2])
        rstd = sb("rstd", [P, PAIRS])
        xn = sb("xn", [P, PAIRS, T])
        q32 = sb("q32", [P, T])
        k32 = sb("k32", [P, T])
        q_parts = sb("q_parts", [P, 2, PAIRS, T], F16)
        k_parts = [sb(f"k_parts{i}", [P, 2, PAIRS, TP], F16) for i in range(2)]
        q_diag = [sb(f"q_diag{i}", [P, 2 * PAIRS * NU, H, QB], F16) for i in range(2)]
        v32 = sb("v32", [P, 2, TP])
        vt32 = sb("vt32", [P, 2 * NU * KB])
        v_parts = sb("v_parts", [P, 2, 2 * NU * KB], F16)
        v_diag = sb("v_diag", [P, 2 * 2, NU, NB, KB], F16)
        row_max = sb("row_max", [P, S_BANKS, 16], BF16)
        probs = sb("probs", [P, NU // OCT, OCT, NB, KB])
        tree = sb("tree", [P, 16, 30])
        row_sum = sb("row_sum", [P, 2, 16])
        inv_sum = sb("inv_sum", [P, 2, 16])
        pt = sb("pt", [P, 2, 2, 4, P], F16)
        own = sb("own", [P, 512])
        att = sb("att", [P, NQ, 2, 64])
        xr_sb = sb("xr_sb", [P, PAIRS, T])
        x1 = sb("x1", [P, PAIRS, T])
        stats2 = sb("stats2", [P, PAIRS, 6])
        mean_var2 = sb("mean_var2", [P, PAIRS, 2])
        rstd2 = sb("rstd2", [P, PAIRS])
        minus_half = sb("minus_half", [P, PAIRS])
        eps = sb("eps", [P, PAIRS])
        gate = sb("gate", [P, 1])
        x2 = sb("x2", [P, PAIRS, T])
        x2_parts = sb("x2_parts", [P, PAIRS, 2, T], F16)
        x2t = sb("x2t", [P, PAIRS, 2 * KC * P], F16)
        ff16 = sb("ff16", [P, T], F16)
        ffb = sb("ffb", [P, T], F16)

        wq_t = sb("wq_t", [P, P])
        wk_t = sb("wk_t", [P, P])
        wv_t = sb("wv_t", [P, P])
        wo_t = sb("wo_t", [P, 4, P])
        bq_sb = sb("bq_sb", [P, 1])
        bk_sb = sb("bk_sb", [P, 1])
        bv_sb = sb("bv_sb", [P, 2])
        bo_sb = sb("bo_sb", [P, 1])
        bias_sb = sb("bias_sb", [P, OUT_F], F16)
        ident = sb("ident", [P, P])
        ident16 = sb("ident16", [P, P], F16)
        minus_ident = sb("minus_ident", [P, P], BF16)
        row_pick = sb("row_pick", [P, P], BF16)
        window = sb("window", [P, 16, KB], BF16)
        head_of_row = sb("head_of_row", [P, H])
        head_of_col = sb("head_of_col", [P, 4])
        batch_of_row = sb("batch_of_row", [P, NB])
        w_ffn = sb("w_ffn", [P, KC, OUT_F], F16)

        scratch = v_diag[:, :, :, :, :].rearrange("p a u b c -> p (a u b c)")
        early = probs[:, :, :, :, :].rearrange("p o u b w -> p (o u b w)")
        wq_in, wk_in, wv_in = (early[:, n * P:(n + 1) * P] for n in range(3))
        wo_in = early[:, 4 * P:8 * P].rearrange("p (n c) -> p n c", c=P)

        def carve(at, n, dt):
            size = {I32: 2, F32: 2, F16: 1}[dt]
            return scratch[:, at:at + n * size].bitcast(dt)

        part_i = carve(0, 4, I32)
        part_f = carve(8, 4, F32)
        col_i = carve(16, P, I32)
        col_f = carve(16 + 256, P, F32)
        t_i = carve(16 + 512, P, I32)
        t_f = carve(16 + 768, P, F32)
        lo_f = carve(16 + 1024, KB, F32)
        hi_f = carve(16 + 1088, KB, F32)
        shift_i = carve(16 + 1152, 2, I32)
        word_i = carve(2048, KC * OUT_F, I32)
        nib_i = carve(2048 + 4096, KC * OUT_F, I32)
        z_in = carve(2048 + 8192, OUT_F // NIB, I32)
        z_i = carve(2048 + 8192 + 128, OUT_F, I32)
        g_i = carve(2048 + 9216 + 256, IN_F, I32)
        g_f = carve(2048 + 10240 + 256, IN_F, F32)
        gneg_f = carve(2048 + 11264 + 256, IN_F, F32)
        q4_in = q_diag[1][:, :, :, :].rearrange("p a b c -> p (a b c)")
        nib_f = q4_in[:, 0:2 * KC * OUT_F].bitcast(F32)
        lev_h = q4_in[:, 4096:4096 + KC * OUT_F]
        z_h = q4_in[:, 8192:8192 + OUT_F]
        s_h = q4_in[:, 8704:8704 + OUT_F]
        hot_h = q4_in[:, 9216:9216 + IN_F]

        ps_s = [ps(f"ps_s{i}") for i in range(S_BANKS)]
        ps_t = [ps(f"ps_t{i}") for i in range(2)]
        ps_o = ps("ps_o")
        ps_m = [ps(f"ps_m{i}") for i in range(2)]

        setup_loaded = sem("setup_loaded")
        setup_zeroed = sem("setup_zeroed")
        iotas = sem("iotas")
        consts = sem("consts")
        setup_pe = sem("setup_pe")
        wt_copied = sem("wt_copied")
        x_in = sem("x_in")
        c_in = sem("c_in")
        xr_in = sem("xr_in")
        stored = [sem(f"stored{i}") for i in range(PAIRS)]
        half_ready = sem("half_ready")
        x_stats = sem("x_stats")
        x_var = sem("x_var")
        x_rstd = sem("x_rstd")
        x1_stats = sem("x1_stats")
        x1_var = sem("x1_var")
        x1_rstd = sem("x1_rstd")
        xn_ready = sem("xn_ready")
        q_done = sem("q_done")
        k_done = sem("k_done")
        v_done = sem("v_done")
        q_out = sem("q_out")
        k_out = sem("k_out")
        v_out = sem("v_out")
        q_rest = sem("q_rest")
        k_rest = sem("k_rest")
        q_diag_ready = sem("q_diag_ready")
        vt_ready = sem("vt_ready")
        v_main = sem("v_main")
        v_rest = sem("v_rest")
        v_diag_ready = sem("v_diag_ready")
        scored = sem("scored")
        maxed = sem("maxed")
        shifted = sem("shifted")
        exped = sem("exped")
        summing = sem("summing")
        inverted = sem("inverted")
        normed = sem("normed")
        turned = sem("turned")
        p_main = sem("p_main")
        p_rest = sem("p_rest")
        valued = sem("valued")
        owned = sem("owned")
        att_ready = sem("att_ready")
        wo_done = sem("wo_done")
        x1_ready = sem("x1_ready")
        x2_ready = sem("x2_ready")
        x2_main = sem("x2_main")
        x2_rest = sem("x2_rest")
        ft_done = sem("ft_done")
        ft_out = sem("ft_out")
        ff_done = sem("ff_done")
        ff_out = sem("ff_out")
        ffb_ready = sem("ffb_ready")
        out_ready = sem("out_ready")

        N_LOADS = 2 * (2 + 2 + 4) + 6 + 2 * NB + 1 + KC + 3

        def x_row(at, view):
            if isinstance(at.i, int):
                return view[2 * at.i + at.k]
            return view[bass.ds(at.i * 2 + at.k, 1), :, :, :].rearrange("n p q t -> (n p) q t")

        def bank_of_probs(k):
            return probs[:, k // 2, :, k % 2:NB:2, :]

        block = es.enter_context(nc.Block())

        @block.sync
        def _(sp):
            def load(at):
                if at.k > 0:
                    sp.wait_ge(xn_ready, at.before(2))
                sp.dma_start(x_sb[:, :, :], x_row(at, x_v)).then_inc(x_in, 16)
                if at.k > 0:
                    sp.wait_ge(k_done, at.before(2))
                    sp.wait_ge(v_done, at.before(2))
                sp.dma_start(c_sb[:, :, :], x_row(at, ctx_v)).then_inc(c_in, 16)

            def load_residual(at):
                sp.wait_ge(x1_ready, at.before(2))
                sp.dma_start(xr_sb[:, :, :], x_row(at, x_v)).then_inc(xr_in, 16)

            def store(at):
                for pr in range(PAIRS):
                    sp.wait_ge(out_ready, at.after(2, pr))
                    sp.dma_start(x_row(at, out_v)[:, pr, :], x1[:, pr, :]).then_inc(stored[pr], 16)

            load(Step(0, 0))
            sp.wait_ge(setup_zeroed, 4)
            for b in range(2):
                r = slice(b * C, (b + 1) * C)
                sp.dma_start(wq_in[r, r], wq).then_inc(setup_loaded, 16)
                sp.dma_start(wk_in[r, r], wk).then_inc(setup_loaded, 16)
                for half in range(2):
                    rows = slice(half * 64 + b * 32, half * 64 + b * 32 + 32)
                    sp.dma_start(wv_in[rows, r], wv[half * 32:half * 32 + 32, :]).then_inc(setup_loaded, 16)
                    for pr in range(PAIRS):
                        cols = slice((2 * pr + b) * 32, (2 * pr + b) * 32 + 32)
                        sp.dma_start(wo_in[r, 2 * pr + half, cols],
                                     wo[:, half * 32:half * 32 + 32]).then_inc(setup_loaded, 16)
            for b in range(2):
                r = slice(b * C, (b + 1) * C)
                sp.dma_start(bq_sb[r, :], bq.unsqueeze(1)).then_inc(setup_loaded, 16)
                sp.dma_start(bk_sb[r, :], bk.unsqueeze(1)).then_inc(setup_loaded, 16)
                sp.dma_start(bo_sb[r, :], bo.unsqueeze(1)).then_inc(setup_loaded, 16)
            for b in range(NB):
                for half in range(2):
                    sp.dma_start(bv_sb[b * 32:b * 32 + 32, half:half + 1],
                                 bv[half * 32:half * 32 + 32].unsqueeze(1)).then_inc(setup_loaded, 16)
            sp.dma_start(bias_sb[:, :], bias.unsqueeze(0).broadcast_to([P, OUT_F])).then_inc(setup_loaded, 16)
            for c in range(KC):
                words = qweight[c * 16:(c + 1) * 16, :].unsqueeze(1).broadcast_to([16, NIB, OUT_F])
                sp.dma_start(word_i[:, c * OUT_F:(c + 1) * OUT_F], words).then_inc(setup_loaded, 16)
            sp.dma_start(z_in[0:GROUPS, :], qzeros).then_inc(setup_loaded, 16)
            sp.dma_start(s_h[0:GROUPS, :], scales).then_inc(setup_loaded, 16)
            sp.dma_start(g_i[0:GROUPS, :], g_idx.unsqueeze(0).broadcast_to([GROUPS, IN_F])).then_inc(setup_loaded, 16)
            load(Step(0, 1))
            load(Step(0, 2))
            load_residual(Step(0, 0))
            with sp.Fori(0, (STEPS - 4) // 2) as i:
                for k in (3, 4):
                    load(Step(i, k))
                    load_residual(Step(i, k - 2))
                    store(Step(i, k - 3))
            load(Step(0, STEPS - 1))
            load_residual(Step(0, STEPS - 3))
            store(Step(0, STEPS - 4))
            load_residual(Step(0, STEPS - 2))
            store(Step(0, STEPS - 3))
            load_residual(Step(0, STEPS - 1))
            store(Step(0, STEPS - 2))
            store(Step(0, STEPS - 1))
            for pr in range(PAIRS):
                sp.wait_ge(stored[pr], 16 * STEPS)

        @block.gpsimd
        def _(pool):
            for tile in (wq_in, wk_in, wv_in):
                pool.memset(tile[:, :], 0.0).then_inc(setup_zeroed, 1)
            pool.memset(wo_in[:, :, :], 0.0).then_inc(setup_zeroed, 1)
            pool.iota(part_i[:, 0:1], pattern=[[0, 1]], base=0, channel_multiplier=1).then_inc(iotas, 1)
            pool.iota(col_i[:, :], pattern=[[1, P]], base=0, channel_multiplier=0).then_inc(iotas, 1)
            pool.iota(t_i[:, :], pattern=[[0, H], [1, QB]], base=0, channel_multiplier=0).then_inc(iotas, 1)

            pool.memset(minus_half[:, :], -0.5).then_inc(half_ready, 1)
            pool.memset(eps[:, :], EPS).then_inc(half_ready, 1)
            pool.wait_ge(half_ready, 2)

            def root(at, mv, var_done, rs, rs_done):
                pool.wait_ge(var_done, at.after(2, 1))
                pool.tensor_tensor(rs[:, :], mv[:, :, 1], eps[:, :], ALU.add).then_inc(rs_done, 1)
                pool.wait_ge(rs_done, at.after(2, 0))
                pool.tensor_tensor(rs[:, :], rs[:, :], minus_half[:, :], ALU.pow).then_inc(rs_done, 1)

            def rest_of_pair(at, pr):
                pool.wait_ge(q_out, at.after(2, pr))
                if pr == 0:
                    pool.wait_ge(q_diag_ready, at.before(1))
                pool.tensor_tensor(q_parts[:, 1, pr, :], q32[:, :], q_parts[:, 0, pr, :],
                                   ALU.subtract).then_inc(q_rest, 1)
                pool.wait_ge(k_out, at.after(2, pr))
                real = slice(LEFT, LEFT + T)
                pool.tensor_tensor(k_parts[at.par][:, 1, pr, real], k32[:, :],
                                   k_parts[at.par][:, 0, pr, real], ALU.subtract).then_inc(k_rest, 1)

            def rest_of_v(at):
                pool.wait_ge(v_main, at.after(1))
                pool.tensor_tensor(v_parts[:, 1, :], vt32[:, :], v_parts[:, 0, :],
                                   ALU.subtract).then_inc(v_rest, 1)

            def sum_rows(at, k):
                pool.wait_ge(exped, at.after(8, k))
                src, width, lo = bank_of_probs(k), KB // 2, 0
                for level in range(LEVELS):
                    a, b = src[..., 0:width], src[..., width:2 * width]
                    if level:
                        pool.wait_ge(summing, at.after(8 * LEVELS, LEVELS * k + level - 1))
                    if level == LEVELS - 1:
                        if at.k > 0 or k >= 2:
                            pool.wait_ge(inverted, at.before(8) + k - 1)
                        dst = row_sum[:, k % 2, :].unsqueeze(2)
                    else:
                        dst = tree[:, :, lo:lo + width]
                        src = dst
                    if level == 0:
                        dst = dst.rearrange("p (u q) w -> p u q w", q=PAIRS)
                    pool.tensor_tensor(dst, a, b, ALU.add).then_inc(summing, 1)
                    lo += width
                    width //= 2

            def normalise(at, k):
                pool.wait_ge(inverted, at.after(8, k))
                src = bank_of_probs(k)
                inv = inv_sum[:, k % 2, :].rearrange("p (u q) -> p u q", q=PAIRS)
                pool.tensor_tensor(src, src, inv.unsqueeze(3).broadcast_to([P, OCT, PAIRS, KB]),
                                   ALU.mult).then_inc(normed, 1)

            def step(at, prev, cur, nxt):
                for s in range(SLOTS):
                    if s >= 1 and cur:
                        sum_rows(at, s - 1)
                    if s == 0 and prev:
                        sum_rows(at.shift(-1), 7)
                    if s >= 2 and cur:
                        normalise(at, s - 2)
                    if s < 2 and prev:
                        normalise(at.shift(-1), s + 6)
                    if nxt and s == 0:
                        root(at.shift(1), mean_var, x_var, rstd, x_rstd)
                    if prev and s == 5:
                        root(at.shift(-1), mean_var2, x1_var, rstd2, x1_rstd)
                    if nxt and s == 3:
                        rest_of_pair(at.shift(1), 0)
                    if nxt and s == 4:
                        rest_of_pair(at.shift(1), 1)
                    if nxt and s == 6:
                        rest_of_v(at.shift(1))

            root(Step(0, 0), mean_var, x_var, rstd, x_rstd)
            rest_of_pair(Step(0, 0), 0)
            rest_of_pair(Step(0, 0), 1)
            rest_of_v(Step(0, 0))
            run_steps(pool, step)

        @block.scalar
        def _(act):
            act.wait_ge(setup_loaded, 16 * N_LOADS)

            def q_and_k_out(at, pr):
                act.wait_ge(q_done, at.after(2, pr))
                if not (at.k == 0 and pr == 0):
                    act.wait_ge(q_rest, at.before(2) + pr)
                if not at.k == 0 and pr == 0:
                    act.wait_ge(q_diag_ready, at.before(1))
                act.activation(q32[:, :], ps_m[0][:, :], ACT.Identity, bias=bq_sb[:, 0:1])
                act.activation(q_parts[:, 0, pr, :], ps_m[0][:, :], ACT.Identity,
                               bias=bq_sb[:, 0:1]).then_inc(q_out, 1)
                act.wait_ge(k_done, at.after(2, pr))
                if not (at.k == 0 and pr == 0):
                    act.wait_ge(k_rest, at.before(2) + pr)
                act.activation(k32[:, :], ps_m[1][:, :], ACT.Identity, bias=bk_sb[:, 0:1])
                act.activation(k_parts[at.par][:, 0, pr, LEFT:LEFT + T], ps_m[1][:, :], ACT.Identity,
                               bias=bk_sb[:, 0:1]).then_inc(k_out, 1)

            def v_half_out(at, half):
                act.wait_ge(v_done, at.after(2, half))
                act.wait_ge(vt_ready, at.before(2))
                act.activation(v32[:, half, LEFT:LEFT + T], ps_m[half][:, :], ACT.Identity,
                               bias=bv_sb[:, half:half + 1]).then_inc(v_out, 1)

            def main_of_v(at):
                act.wait_ge(vt_ready, at.after(2, 1))
                act.wait_ge(v_diag_ready, at.before(2))
                act.activation(v_parts[:, 0, :], vt32[:, :], ACT.Copy).then_inc(v_main, 1)

            def exp_bank(at, k):
                act.wait_ge(shifted, at.after(8, k))
                if at.k > 0:
                    act.wait_ge(turned, at.shift(-1).after(8, 2 * (k // 2) + 1))
                act.activation(bank_of_probs(k),
                               ps_s[k % S_BANKS][:, :].rearrange("p (u q w) -> p u q w", q=PAIRS, w=KB),
                               ACT.Exp, scale=float(HD) ** -0.5).then_inc(exped, 1)

            def main_of_probs(at, q):
                act.wait_ge(turned, at.after(8, q))
                if at.k > 0 or q >= 2:
                    act.wait_ge(valued, at.before(8) + q - 1)
                act.activation(pt[:, q % 2, 0, :, :],
                               ps_t[q % 2][:, :].rearrange("p (u c) -> p u c", c=P), ACT.Copy).then_inc(p_main, 1)

            def main_of_x2(at, pr):
                act.wait_ge(x2_ready, at.after(2, pr))
                act.wait_ge(ft_done, at.before(2) + pr)
                act.activation(x2_parts[:, pr, 0, :], x2[:, pr, :], ACT.Copy).then_inc(x2_main, 1)

            def x2_turned_out(at, pr):
                act.wait_ge(ft_done, at.after(2, pr))
                act.wait_ge(ff_done, at.before(2) + pr)
                act.activation(x2t[:, pr, :], ps_m[pr][:, :].bitcast(F16), ACT.Copy).then_inc(ft_out, 1)

            def ffn_out(at, pr):
                act.wait_ge(ff_done, at.after(2, pr))
                act.wait_ge(ffb_ready, at.before(2) + pr)
                act.activation(ff16[:, :], ps_m[pr][:, :], ACT.Copy).then_inc(ff_out, 1)

            def step(at, prev, cur, nxt):
                for s in range(SLOTS):
                    if s >= 1 and cur:
                        exp_bank(at, s - 1)
                    if s == 0 and prev:
                        exp_bank(at.shift(-1), 7)
                    if nxt and s in (2, 3):
                        q_and_k_out(at.shift(1), s - 2)
                    if s >= T_LAG and cur:
                        main_of_probs(at, s - T_LAG)
                    if s < T_LAG and prev:
                        main_of_probs(at.shift(-1), s + SLOTS - T_LAG)
                    if nxt and s == 4:
                        v_half_out(at.shift(1), 0)
                        v_half_out(at.shift(1), 1)
                    if nxt and s == 6:
                        main_of_v(at.shift(1))
                    if prev and s == 6:
                        main_of_x2(at.shift(-1), 0)
                        main_of_x2(at.shift(-1), 1)
                    if prev and s == 7:
                        for pr in range(PAIRS):
                            x2_turned_out(at.shift(-1), pr)
                        for pr in range(PAIRS):
                            ffn_out(at.shift(-1), pr)

            q_and_k_out(Step(0, 0), 0)
            q_and_k_out(Step(0, 0), 1)
            v_half_out(Step(0, 0), 0)
            v_half_out(Step(0, 0), 1)
            main_of_v(Step(0, 0))
            run_steps(act, step)

        @block.vector
        def _(dve):
            done = [0]

            def in_order(instruction):
                done[0] += 1
                instruction.then_inc(consts, 1)
                dve.wait_ge(consts, done[0])

            for par in range(2):
                in_order(dve.memset(k_parts[par][:, :, :, :], 0.0))
            in_order(dve.memset(v32[:, :, :], 0.0))
            dve.wait_ge(iotas, 3)
            in_order(dve.tensor_scalar(part_i[:, 1:2], part_i[:, 0:1], 63, None, ALU.bitwise_and))
            in_order(dve.tensor_scalar(part_i[:, 2:3], part_i[:, 1:2], 3, None, ALU.logical_shift_right))
            in_order(dve.tensor_scalar(part_i[:, 3:4], part_i[:, 0:1], 5, None, ALU.logical_shift_right))
            in_order(dve.tensor_scalar(shift_i[:, 0:1], part_i[:, 0:1], 7, 2, ALU.bitwise_and,
                                       ALU.logical_shift_left))
            in_order(dve.tensor_scalar(shift_i[:, 1:2], part_i[:, 0:1], 31, 3, ALU.bitwise_and,
                                       ALU.logical_shift_right))
            in_order(dve.tensor_copy(part_f[:, :], part_i[:, :]))
            in_order(dve.tensor_copy(col_f[:, :], col_i[:, :]))
            in_order(dve.tensor_copy(t_f[:, :], t_i[:, :]))
            in_order(dve.tensor_scalar(ident[:, :], col_f[:, :], part_f[:, 0:1], None, ALU.is_equal))
            in_order(dve.tensor_scalar(minus_ident[:, :], ident[:, :], -1.0, None, ALU.mult))
            in_order(dve.tensor_copy(ident16[:, :], ident[:, :]))
            in_order(dve.tensor_scalar(row_pick[:, :], t_f[:, :], part_f[:, 1:2], None, ALU.is_equal))
            in_order(dve.tensor_scalar(head_of_row[:, :], col_f[:, 0:H], part_f[:, 2:3], None, ALU.is_equal))
            in_order(dve.tensor_scalar(batch_of_row[:, :], col_f[:, 0:NB], part_f[:, 3:4], None, ALU.is_equal))
            in_order(dve.tensor_scalar(t_f[:, 0:KB], col_f[:, 0:KB], part_f[:, 1:2], None, ALU.subtract))
            in_order(dve.tensor_scalar(lo_f[:, :], t_f[:, 0:KB], 0.0, MASKED, ALU.is_lt, ALU.mult))
            in_order(dve.tensor_scalar(hi_f[:, :], t_f[:, 0:KB], float(WIN - 1), MASKED, ALU.is_gt, ALU.mult))
            in_order(dve.tensor_tensor(lo_f[:, :], lo_f[:, :], hi_f[:, :], ALU.add))
            in_order(dve.tensor_copy(window[:, :, :], lo_f[:, :].unsqueeze(1).broadcast_to([P, 16, KB])))
            in_order(dve.tensor_copy(part_f[:, 0:1], shift_i[:, 1:2]))
            in_order(dve.tensor_scalar(head_of_col[:, :], col_f[:, 0:4], part_f[:, 0:1], None, ALU.is_equal))

            dve.wait_ge(setup_loaded, 16 * N_LOADS)
            in_order(dve.tensor_copy(part_f[:, 0:1], part_i[:, 0:1]))
            zi = z_i[0:GROUPS, :].rearrange("g (w j) -> g w j", j=NIB)
            for j in range(NIB):
                in_order(dve.tensor_scalar(zi[:, :, j], z_in[0:GROUPS, :], 4 * j, 15,
                                           ALU.logical_shift_right, ALU.bitwise_and))
            in_order(dve.tensor_copy(z_h[0:GROUPS, :], z_i[0:GROUPS, :]))
            g, neg = g_f[0:GROUPS, :], gneg_f[0:GROUPS, :]
            in_order(dve.tensor_copy(g, g_i[0:GROUPS, :]))
            in_order(dve.tensor_scalar(neg, g, 0.0, float(GROUPS), ALU.is_lt, ALU.mult))
            in_order(dve.tensor_tensor(g, g, neg, ALU.add))
            in_order(dve.tensor_scalar(g, g, 0.0, float(GROUPS - 1), ALU.max, ALU.min))
            in_order(dve.tensor_scalar(hot_h[0:GROUPS, :], g, part_f[0:GROUPS, 0:1], None, ALU.is_equal))
            hot_at = done[0]
            in_order(dve.tensor_tensor(nib_i[:, :], word_i[:, :],
                                       shift_i[:, 0:1].broadcast_to([P, KC * OUT_F]),
                                       ALU.logical_shift_right))
            in_order(dve.tensor_scalar(nib_i[:, :], nib_i[:, :], 15, None, ALU.bitwise_and))
            in_order(dve.tensor_copy(nib_f[:, :], nib_i[:, :]))
            for c in range(KC):
                cols = slice(c * OUT_F, (c + 1) * OUT_F)
                dve.wait_ge(setup_pe, 2 * c + 1)
                in_order(dve.tensor_tensor(lev_h[:, cols], nib_f[:, cols], ps_t[0][:, :], ALU.subtract))
                dve.wait_ge(setup_pe, 2 * c + 2)
                in_order(dve.tensor_tensor(w_ffn[:, c, :], lev_h[:, cols], ps_t[1][:, :], ALU.mult))
            dve.wait_ge(setup_pe, 2 * KC + 1)
            for n, tile in enumerate((wq_t, wk_t, wv_t)):
                dve.tensor_copy(tile[:, :], ps_m[0][:, n * P:(n + 1) * P]).then_inc(wt_copied, 1)
            dve.wait_ge(setup_pe, 2 * KC + 2)
            dve.tensor_copy(wo_t[:, :, :], ps_m[1][:, :].rearrange("p (n c) -> p n c", c=P)).then_inc(wt_copied, 1)
            assert hot_at == HOT_AT, hot_at

            def moments(at, src, st, stats_done, mv, var_done):
                for pr in range(PAIRS):
                    dve.bn_stats(st[:, pr, :], src[:, pr, :]).then_inc(stats_done, 1)
                dve.wait_ge(stats_done, at.after(2, 1))
                dve.memset(gate[:, :], 0.0)
                for pr in range(PAIRS):
                    dve.bn_aggr(mv[:, pr, :], st[:, pr, :]).then_inc(var_done, 1)

            def normed_rows(at, src, dst, mv, rs, ready):
                for pr in range(PAIRS):
                    dve.tensor_scalar(dst[:, pr, :], src[:, pr, :], mv[:, pr, 0:1], rs[:, pr:pr + 1],
                                      ALU.subtract, ALU.mult).then_inc(ready, 1)

            def moments_x(at):
                dve.wait_ge(x_in, at.before(16) + 16)
                moments(at, x_sb, stats, x_stats, mean_var, x_var)

            def norm_x(at):
                dve.wait_ge(x_rstd, at.after(2, 1))
                dve.wait_ge(q_done, at.before(2))
                normed_rows(at, x_sb, xn, mean_var, rstd, xn_ready)

            def q_diagonals(at, heads):
                if heads[0] == 0:
                    dve.wait_ge(q_rest, at.after(2, 1))
                    if at.k >= 2:
                        dve.wait_ge(scored, at.shift(-1).before(8))
                src = q_parts[:, :, :, :].rearrange("p a q t -> p (a q t)").rearrange("p (u t) -> p u t", t=QB)
                for h in heads:
                    op = dve.tensor_scalar(q_diag[at.par][:, :, h, :], src, head_of_row[:, h:h + 1], None, ALU.mult)
                if heads[-1] == H - 1:
                    op.then_inc(q_diag_ready, 1)

            def turn_v(at, half):
                dve.wait_ge(v_out, at.after(2, half))
                if half == 0:
                    dve.wait_ge(v_rest, at.before(1))
                keys = v32[:, half, :]
                src = bass.AP(keys.tensor, keys.offset, [keys.ap[0], [QB, NU], [1, KB]])
                dst = vt32[:, half * NU * KB:(half + 1) * NU * KB].rearrange("p (u c) -> p u c", c=KB)
                dve.transpose(dst, src).then_inc(vt_ready, 1)

            def v_diagonals(at, part):
                dve.wait_ge(v_rest, at.after(1))
                dve.wait_ge(valued, at.before(8) - (4 if part == 0 and at.k else 0))
                blocks = slice(part * NU // 2, (part + 1) * NU // 2)
                src = v_parts[:, :, :].rearrange("p a (f u c) -> p (a f) u c", f=2, c=KB)[:, :, blocks, :]
                for b in range(NB):
                    op = dve.tensor_scalar(v_diag[:, :, blocks, b, :], src, batch_of_row[:, b:b + 1], None, ALU.mult)
                op.then_inc(v_diag_ready, 1)

            def maxima(at, k):
                dve.wait_ge(scored, at.after(8, k))
                dve.tensor_reduce(row_max[:, k % S_BANKS, :],
                                  ps_s[k % S_BANKS][:, :].rearrange("p (c w) -> p c w", w=KB),
                                  AX.X, ALU.max).then_inc(maxed, 1)

            def invert(at, k):
                dve.wait_ge(summing, at.after(8 * LEVELS, LEVELS * k + LEVELS - 1))
                if at.k > 0 or k >= 2:
                    dve.wait_ge(normed, at.before(8) + k - 1)
                dve.reciprocal(inv_sum[:, k % 2, :], row_sum[:, k % 2, :]).then_inc(inverted, 1)

            def rest_of_probs(at, q):
                dve.wait_ge(p_main, at.after(8, q))
                dve.tensor_tensor(pt[:, q % 2, 1, :, :], ps_t[q % 2][:, :].rearrange("p (u c) -> p u c", c=P),
                                  pt[:, q % 2, 0, :, :], ALU.subtract).then_inc(p_rest, 1)

            def own_heads(at, q):
                dve.wait_ge(valued, at.after(8, q))
                if at.k > 0 or q > 0:
                    dve.wait_ge(att_ready, at.before(8) + q)
                mask = head_of_col[:, :].unsqueeze(1).unsqueeze(3).broadcast_to([P, 8, 4, QB])
                dve.tensor_tensor(own[:, :].rearrange("p (a h t) -> p a h t", h=4, t=QB),
                                  ps_o[:, :].rearrange("p (a h t) -> p a h t", h=4, t=QB),
                                  mask, ALU.mult).then_inc(owned, 1)
                dve.wait_ge(owned, at.after(8, q))
                if q == 0:
                    dve.wait_ge(wo_done, at.before(2))
                dve.tensor_reduce(att[:, q, :, :].rearrange("p f (u t) -> p (f u) t", t=QB),
                                  own[:, :].rearrange("p (a h t) -> p a t h", h=4, t=QB),
                                  AX.X, ALU.add).then_inc(att_ready, 1)

            def residual(at):
                dve.wait_ge(xr_in, at.before(16) + 16)
                for pr in range(PAIRS):
                    dve.wait_ge(wo_done, at.after(2, pr))
                    dve.wait_ge(stored[pr], at.before(16))
                    dve.scalar_tensor_tensor(x1[:, pr, :], ps_m[pr][:, :], bo_sb[:, 0:1], xr_sb[:, pr, :],
                                             ALU.add, ALU.add).then_inc(x1_ready, 1)

            def moments_x1(at):
                dve.wait_ge(x1_ready, at.after(2, 1))
                moments(at, x1, stats2, x1_stats, mean_var2, x1_var)

            def norm_x1(at):
                dve.wait_ge(x1_rstd, at.after(2, 1))
                normed_rows(at, x1, x2, mean_var2, rstd2, x2_ready)

            def rest_of_x2(at, pr):
                dve.wait_ge(x2_main, at.after(2, pr))
                dve.wait_ge(x2_ready, at.after(2, pr))
                dve.tensor_tensor(x2_parts[:, pr, 1, :], x2[:, pr, :], x2_parts[:, pr, 0, :],
                                  ALU.subtract).then_inc(x2_rest, 1)

            def outputs(at, pr):
                dve.wait_ge(ff_out, at.after(2, pr))
                dve.wait_ge(out_ready, at.before(2) + pr)
                dve.tensor_tensor(ffb[:, :], ff16[:, :], bias_sb[:, :], ALU.add).then_inc(ffb_ready, 1)
                dve.wait_ge(ffb_ready, at.after(2, pr))
                dve.tensor_tensor(x1[:, pr, :], x1[:, pr, :], ffb[:, :], ALU.add).then_inc(out_ready, 1)

            def step(at, prev, cur, nxt):
                for s in range(SLOTS):
                    if cur:
                        maxima(at, s)
                    if s >= 2 and cur:
                        invert(at, s - 2)
                    if s < 2 and prev:
                        invert(at.shift(-1), s + 6)
                    if nxt and s == 0:
                        moments_x(at.shift(1))
                    if s >= T_LAG and cur:
                        rest_of_probs(at, s - T_LAG)
                    if s < T_LAG and prev:
                        rest_of_probs(at.shift(-1), s + SLOTS - T_LAG)
                    if s >= AV_LAG and cur:
                        own_heads(at, s - AV_LAG)
                    if s < AV_LAG and prev:
                        own_heads(at.shift(-1), s + SLOTS - AV_LAG)
                    if nxt and s == 0:
                        norm_x(at.shift(1))
                    if nxt and s == 4:
                        q_diagonals(at.shift(1), range(0, 3))
                    if nxt and s == 5:
                        turn_v(at.shift(1), 0)
                        turn_v(at.shift(1), 1)
                        q_diagonals(at.shift(1), range(3, 6))
                    if nxt and s == 6:
                        q_diagonals(at.shift(1), range(6, H))
                    if cur and s in (2, 5):
                        v_diagonals(at, s // 4)
                    if prev and s == 5:
                        residual(at.shift(-1))
                        moments_x1(at.shift(-1))
                    if prev and s == 6:
                        norm_x1(at.shift(-1))
                        rest_of_x2(at.shift(-1), 0)
                        rest_of_x2(at.shift(-1), 1)
                    if prev and s == 7:
                        outputs(at.shift(-1), 0)
                        outputs(at.shift(-1), 1)

            first = Step(0, 0)
            moments_x(first)
            norm_x(first)
            turn_v(first, 0)
            turn_v(first, 1)
            q_diagonals(first, range(H))
            run_steps(dve, step)

        @block.tensor
        def _(pe):
            pe.wait_ge(consts, HOT_AT)
            for c in range(KC):
                hot = hot_h[0:GROUPS, c * P:(c + 1) * P]
                if c:
                    pe.wait_ge(consts, HOT_AT + 3 + 2 * (c - 1) + 1)
                pe.matmul(ps_t[0][:, :], hot, z_h[0:GROUPS, :], start=True, stop=True).then_inc(setup_pe, 1)
                if c:
                    pe.wait_ge(consts, HOT_AT + 3 + 2 * (c - 1) + 2)
                pe.matmul(ps_t[1][:, :], hot, s_h[0:GROUPS, :], start=True, stop=True).then_inc(setup_pe, 1)
            pe.wait_ge(setup_loaded, 16 * N_LOADS)
            for n, tile in enumerate((wq_in, wk_in, wv_in)):
                last = pe.transpose(ps_m[0][:, n * P:(n + 1) * P], tile[:, :], ident[:, :])
            last.then_inc(setup_pe, 1)
            for n in range(4):
                last = pe.transpose(ps_m[1][:, n * P:(n + 1) * P], wo_in[:, n, :], ident[:, :])
            last.then_inc(setup_pe, 1)
            pe.wait_ge(wt_copied, 4)

            def project_q_k(at, pr):
                pe.wait_ge(xn_ready, at.after(2, pr))
                if pr == 0 and at.k > 0:
                    pe.wait_ge(v_out, at.before(2))
                    if at.k > 2:
                        pe.wait_ge(ff_out, at.shift(-2).before(2))
                if pr == 1:
                    pe.wait_ge(q_out, at.after(2, 0))
                pe.matmul(ps_m[0][:, :], wq_t[:, :], xn[:, pr, :], start=True, stop=True).then_inc(q_done, 1)
                if pr == 0:
                    pe.wait_ge(c_in, at.before(16) + 16)
                if pr == 1:
                    pe.wait_ge(k_out, at.after(2, 0))
                pe.matmul(ps_m[1][:, :], wk_t[:, :], c_sb[:, pr, :],
                          start=True, stop=True).then_inc(k_done, 1)

            def project_v(at, half):
                pe.wait_ge(k_out if half else q_out, at.after(2, 1))
                for pr in range(PAIRS):
                    last = pe.matmul(ps_m[half][pr * 64:pr * 64 + 64, :], wv_t[:, half * 64:half * 64 + 64],
                                     c_sb[:, pr, :], start=True, stop=True)
                last.then_inc(v_done, 1)

            def scores(at, k):
                octet, side = k // 2, k % 2
                bank = ps_s[k % S_BANKS]
                if k == 0:
                    pe.wait_ge(q_diag_ready, at.after(1))
                    pe.wait_ge(k_rest, at.after(2, 1))
                if k >= S_BANKS:
                    pe.wait_ge(exped, at.after(8, k - S_BANKS))
                elif at.k > 0:
                    pe.wait_ge(exped, at.shift(-1).after(8, LAST_ON_BANK[k]))
                rows = slice(side * 64, side * 64 + 64)
                pe.matmul(bank[:, :], row_pick[rows, :],
                          window[rows, :, :].rearrange("p c w -> p (c w)"),
                          start=True, stop=False, skip_group_check=True)
                for u in range(OCT):
                    for pr in range(PAIRS):
                        blk = octet * OCT + u
                        cell = (u * PAIRS + pr) * KB
                        for qp, kp in ((0, 0), (0, 1), (1, 0)):
                            last = pe.matmul(bank[:, cell:cell + KB],
                                             q_diag[at.par][rows, (qp * PAIRS + pr) * NU + blk, :, :]
                                             .rearrange("p h t -> p (h t)"),
                                             k_parts[at.par][rows, kp, pr, blk * QB:blk * QB + KB],
                                             start=False, stop=False, skip_group_check=True)
                last.then_inc(scored, 1)

            def shift_scores(at, k):
                pe.wait_ge(maxed, at.after(8, k))
                pe.matmul(ps_s[k % S_BANKS][:, :].rearrange("p (c w) -> p c w", w=KB), minus_ident[:, :],
                          row_max[:, k % S_BANKS, :].unsqueeze(2).broadcast_to([P, 16, KB]),
                          start=False, stop=True, skip_group_check=True).then_inc(shifted, 1)

            def turn_probs(at, q):
                pe.wait_ge(normed, at.after(8, 2 * (q // 2) + 1))
                if at.k > 0 or q >= 2:
                    pe.wait_ge(p_rest, at.before(8) + q - 1)
                for j in range(4):
                    last = pe.transpose(ps_t[q % 2][:, j * P:(j + 1) * P],
                                        probs[:, q // 2, 4 * (q % 2) + j, :, :].rearrange("p b w -> p (b w)"),
                                        ident[:, :])
                last.then_inc(turned, 1)

            def values(at, q):
                if q in (0, NQ // 2):
                    pe.wait_ge(v_diag_ready, at.after(2, q // (NQ // 2)))
                pe.wait_ge(p_rest, at.after(8, q))
                if at.k > 0 or q > 0:
                    pe.wait_ge(owned, at.before(8) + q)
                for half in range(2):
                    for j in range(4):
                        cell = (half * 4 + j) * 64
                        terms = ((0, 0), (0, 1), (1, 0))
                        for n, (vp, pp) in enumerate(terms):
                            last = pe.matmul(ps_o[:, cell:cell + 64],
                                             v_diag[:, vp * 2 + half, 4 * q + j, :, :]
                                             .rearrange("p b c -> p (b c)"),
                                             pt[:, q % 2, pp, j, half * 64:half * 64 + 64],
                                             start=n == 0, stop=n == len(terms) - 1)
                last.then_inc(valued, 1)

            def project_out(at, nxt):
                pe.wait_ge(att_ready, at.after(8, NQ - 1))
                if nxt:
                    pe.wait_ge(v_out, at.shift(2).after(2, 1))
                else:
                    pe.wait_ge(ff_out, at.before(2))
                for pr in range(PAIRS):
                    for half in range(2):
                        last = pe.matmul(ps_m[pr][:, :], wo_t[:, 2 * pr + half, :],
                                         att[:, :, half, :], start=half == 0, stop=half == 1)
                    last.then_inc(wo_done, 1)

            def turn_x2(at, pr):
                pe.wait_ge(x2_rest, at.after(2, pr))
                for part in range(2):
                    for c in range(KC):
                        n = part * KC + c
                        last = pe.transpose(ps_m[pr][:, :].bitcast(F16)[:, n * P:(n + 1) * P],
                                            x2_parts[:, pr, part, c * P:(c + 1) * P], ident16[:, :])
                last.then_inc(ft_done, 1)

            def feed_forward(at, pr):
                pe.wait_ge(ft_out, at.after(2, pr))
                for n in range(2 * KC):
                    last = pe.matmul(ps_m[pr][:, :], x2t[:, pr, n * P:(n + 1) * P], w_ffn[:, n % KC, :],
                                     start=n == 0, stop=n == 2 * KC - 1)
                last.then_inc(ff_done, 1)

            def step(at, prev, cur, nxt):
                for s in range(SLOTS):
                    if cur:
                        scores(at, s)
                    if s >= 1 and cur:
                        shift_scores(at, s - 1)
                    if s == 0 and prev:
                        shift_scores(at.shift(-1), 7)
                    if s >= T_LAG and cur:
                        turn_probs(at, s - T_LAG)
                    if s < T_LAG and prev:
                        turn_probs(at.shift(-1), s + SLOTS - T_LAG)
                    if prev and s == 5:
                        project_out(at.shift(-1), nxt)
                    if s >= AV_LAG and cur:
                        values(at, s - AV_LAG)
                    if s < AV_LAG and prev:
                        values(at.shift(-1), s + SLOTS - AV_LAG)
                    if nxt and s in (1, 2):
                        project_q_k(at.shift(1), s - 1)
                    if nxt and s == 3:
                        project_v(at.shift(1), 0)
                        project_v(at.shift(1), 1)
                    if prev and s == 7:
                        turn_x2(at.shift(-1), 0)
                        turn_x2(at.shift(-1), 1)
                        feed_forward(at.shift(-1), 0)
                        feed_forward(at.shift(-1), 1)

            first = Step(0, 0)
            project_q_k(first, 0)
            project_q_k(first, 1)
            project_v(first, 0)
            project_v(first, 1)
            run_steps(pe, step)


HOT_AT = 3 + 21 + 1 + NIB + 1 + 5

_INS = ['x', 'ctx_4096', 'L0_xattn_Wq', 'L0_xattn_bq', 'L0_xattn_Wk', 'L0_xattn_bk', 'L0_xattn_Wv', 'L0_xattn_bv',
        'L0_xattn_Wo', 'L0_xattn_bo', 'L0_ffn_qweight', 'L0_ffn_qzeros', 'L0_ffn_scales', 'L0_ffn_g_idx',
        'L0_ffn_bias']


def kernel(**inputs):
    import numpy as _np
    import concourse.bacc as _bacc
    from concourse import mybir as _mybir
    from concourse.bass_utils import run_bass_kernel_spmd as _run

    nc = _bacc.Bacc("TRN2", target_bir_lowering=False, num_devices=1)
    arrays, args = {}, []
    for name in _INS:
        a = _np.ascontiguousarray(inputs[name])
        arrays[f"in_{name}"] = a
        args.append(nc.dram_tensor(f"in_{name}", a.shape, _mybir.dt.from_np(a.dtype), kind="ExternalInput").ap())
    result = nc.dram_tensor("result", (B, C, T), F32, kind="ExternalOutput").ap()
    build(nc, *args, result)
    r = _run(nc, [arrays], core_ids=[0])
    return r.results[0]["result"]
```

```python
from contextlib import ExitStack

import concourse.bass as bass
from concourse import mybir

F32 = mybir.dt.float32
BF16 = mybir.dt.bfloat16
F16 = mybir.dt.float16
I32 = mybir.dt.int32
ALU = mybir.AluOpType
ACT = mybir.ActivationFunctionType
AX = mybir.AxisListType

P = 128
B, C, T = 32, 64, 512
H, WIN = 8, 16
HD = C // H
PAIRS = 2
NB = 2 * PAIRS
STEPS = B // NB
QB = 16
KB = 32
NU = T // QB
LEFT = WIN // 2
TP = (NU - 1) * QB + KB
OCT = 8
NQ = NU // 4
SLOTS = 8
GROUPS, IN_F, OUT_F = 4, 512, 512
NIB = 8
KC = IN_F // P
EPS = 1e-5
MASKED = -1e30
SUM_LAG, NORM_LAG = 1, 2
TURN_LAG, REST_LAG, VALUE_LAG = 4, 5, 6
S_BANKS = 3
LEVELS = 5
LAST_ON_BANK = {0: 6, 1: 7, 2: 5}


class Step:

    def __init__(self, i, k):
        self.i, self.k = i, k
        self.par = k % 2

    def after(self, per, event=0):
        return self.i * (2 * per) + (self.k * per + event + 1)

    def before(self, per):
        return self.i * (2 * per) + self.k * per

    def shift(self, d):
        return Step(self.i, self.k + d)


def run_steps(eng, step):
    step(Step(0, 0), False, False, True, True)
    step(Step(0, 1), False, True, True, True)
    with eng.Fori(0, (STEPS - 4) // 2) as i:
        step(Step(i, 2), True, True, True, True)
        step(Step(i, 3), True, True, True, True)
    step(Step(0, STEPS - 2), True, True, True, True)
    step(Step(0, STEPS - 1), True, True, True, False)
    step(Step(0, STEPS), True, True, False, False)
    step(Step(0, STEPS + 1), True, False, False, False)


def lagged(s, lag, cur, done, at):
    if s >= lag:
        return [(at, s - lag)] if cur else []
    return [(at.shift(-1), s - lag + SLOTS)] if done else []


def build(nc, x, ctx_in, wq, bq, wk, bk, wv, bv, wo, bo, qweight, qzeros, scales, g_idx, bias, out):
    x_v = x.rearrange("(n q b) c t -> n (b c) q t", q=PAIRS, b=2)
    ctx_v = ctx_in.rearrange("(n q b) c t -> n (b c) q t", q=PAIRS, b=2)
    out_v = out.rearrange("(n q b) c t -> n (b c) q t", q=PAIRS, b=2)

    with ExitStack() as es:
        def sb(name, shape, dt=F32):
            return es.enter_context(nc.sbuf_tensor(name, shape, dt))

        def ps(name):
            return es.enter_context(nc.psum_tensor(name, [P, 512], F32))

        def sem(name):
            return es.enter_context(nc.semaphore(name))

        x_sb = sb("x_sb", [P, PAIRS, T])
        c_sb = sb("c_sb", [P, PAIRS, T])
        stats = sb("stats", [P, PAIRS, 6])
        mean_var = sb("mean_var", [P, PAIRS, 2])
        rstd = sb("rstd", [P, PAIRS])
        xn = sb("xn", [P, PAIRS, T])
        q32 = sb("q32", [P, T])
        k32 = sb("k32", [P, T])
        q_parts = sb("q_parts", [P, 2, PAIRS, T], F16)
        k_parts = [sb(f"k_parts{i}", [P, 2, PAIRS, TP], F16) for i in range(2)]
        q_diag = [sb(f"q_diag{i}", [P, 2 * PAIRS * NU, H, QB], F16) for i in range(2)]
        v32 = sb("v32", [P, 2, TP])
        vt32 = sb("vt32", [P, 2 * NU * KB])
        v_parts = sb("v_parts", [P, 2, 2 * NU * KB], F16)
        v_diag = sb("v_diag", [P, 2 * 2, NU, NB, KB], F16)
        row_max = sb("row_max", [P, S_BANKS, 16], BF16)
        probs = sb("probs", [P, NU // OCT, OCT, NB, KB])
        tree = sb("tree", [P, 16, 30])
        row_sum = sb("row_sum", [P, 2, 16])
        inv_sum = sb("inv_sum", [P, 2, 16])
        pt = sb("pt", [P, 2, 2, 4, P], F16)
        own = sb("own", [P, 512])
        att = sb("att", [P, NQ, 2, 64])
        xr_sb = sb("xr_sb", [P, PAIRS, T])
        x1 = sb("x1", [P, PAIRS, T])
        stats2 = sb("stats2", [P, PAIRS, 6])
        mean_var2 = sb("mean_var2", [P, PAIRS, 2])
        rstd2 = sb("rstd2", [P, PAIRS])
        minus_half = sb("minus_half", [P, PAIRS])
        eps = sb("eps", [P, PAIRS])
        gate = sb("gate", [P, 1])
        x2 = sb("x2", [P, PAIRS, T])
        x2_parts = sb("x2_parts", [P, PAIRS, 2, T], F16)
        x2t = sb("x2t", [P, PAIRS, 2 * KC * P], F16)
        ff16 = sb("ff16", [P, PAIRS, T], F16)
        ffb = sb("ffb", [P, T], F16)

        wq_t = sb("wq_t", [P, P])
        wk_t = sb("wk_t", [P, P])
        wv_t = sb("wv_t", [P, P])
        wo_t = sb("wo_t", [P, 4, P])
        bq_sb = sb("bq_sb", [P, 1])
        bk_sb = sb("bk_sb", [P, 1])
        bv_sb = sb("bv_sb", [P, 2])
        bo_sb = sb("bo_sb", [P, 1])
        bias_sb = sb("bias_sb", [P, OUT_F], F16)
        ident = sb("ident", [P, P])
        ident16 = sb("ident16", [P, P], F16)
        minus_ident = sb("minus_ident", [P, P], BF16)
        row_pick = sb("row_pick", [P, P], BF16)
        window = sb("window", [P, 16, KB], BF16)
        head_of_row = sb("head_of_row", [P, H])
        head_of_col = sb("head_of_col", [P, 4])
        batch_of_row = sb("batch_of_row", [P, NB])
        w_ffn = sb("w_ffn", [P, KC, OUT_F], F16)

        scratch = v_diag[:, :, :, :, :].rearrange("p a u b c -> p (a u b c)")
        early = probs[:, :, :, :, :].rearrange("p o u b w -> p (o u b w)")
        wq_in, wk_in, wv_in = (early[:, n * P:(n + 1) * P] for n in range(3))
        wo_in = early[:, 4 * P:8 * P].rearrange("p (n c) -> p n c", c=P)

        def carve(at, n, dt):
            size = {I32: 2, F32: 2, F16: 1}[dt]
            return scratch[:, at:at + n * size].bitcast(dt)

        part_i = carve(0, 4, I32)
        part_f = carve(8, 4, F32)
        col_i = carve(16, P, I32)
        col_f = carve(16 + 256, P, F32)
        t_i = carve(16 + 512, P, I32)
        t_f = carve(16 + 768, P, F32)
        lo_f = carve(16 + 1024, KB, F32)
        hi_f = carve(16 + 1088, KB, F32)
        shift_i = carve(16 + 1152, 2, I32)
        word_i = carve(2048, KC * OUT_F, I32)
        nib_i = carve(2048 + 4096, KC * OUT_F, I32)
        z_in = carve(2048 + 8192, OUT_F // NIB, I32)
        z_i = carve(2048 + 8192 + 128, OUT_F, I32)
        g_i = carve(2048 + 9216 + 256, IN_F, I32)
        g_f = carve(2048 + 10240 + 256, IN_F, F32)
        gneg_f = carve(2048 + 11264 + 256, IN_F, F32)
        q4_in = q_diag[1][:, :, :, :].rearrange("p a b c -> p (a b c)")
        nib_f = q4_in[:, 0:2 * KC * OUT_F].bitcast(F32)
        lev_h = q4_in[:, 4096:4096 + KC * OUT_F]
        z_h = q4_in[:, 8192:8192 + OUT_F]
        s_h = q4_in[:, 8704:8704 + OUT_F]
        hot_h = q4_in[:, 9216:9216 + IN_F]

        ps_s = [ps(f"ps_s{i}") for i in range(S_BANKS)]
        ps_t = [ps(f"ps_t{i}") for i in range(2)]
        ps_o = ps("ps_o")
        ps_m = [ps(f"ps_m{i}") for i in range(2)]

        setup_loaded = sem("setup_loaded")
        setup_zeroed = sem("setup_zeroed")
        iotas = sem("iotas")
        consts = sem("consts")
        setup_pe = sem("setup_pe")
        wt_copied = sem("wt_copied")
        x_in = sem("x_in")
        c_in = sem("c_in")
        xr_in = sem("xr_in")
        stored = [sem(f"stored{i}") for i in range(PAIRS)]
        half_ready = sem("half_ready")
        x_stats = sem("x_stats")
        x_var = sem("x_var")
        x_rstd = sem("x_rstd")
        x1_stats = sem("x1_stats")
        x1_var = sem("x1_var")
        x1_rstd = sem("x1_rstd")
        xn_ready = sem("xn_ready")
        q_done = sem("q_done")
        k_done = sem("k_done")
        v_done = sem("v_done")
        q_out = sem("q_out")
        k_out = sem("k_out")
        v_out = sem("v_out")
        q_rest = sem("q_rest")
        k_rest = sem("k_rest")
        q_diag_ready = sem("q_diag_ready")
        vt_ready = sem("vt_ready")
        v_main = sem("v_main")
        v_rest = sem("v_rest")
        v_diag_ready = sem("v_diag_ready")
        scored = sem("scored")
        maxed = sem("maxed")
        shifted = sem("shifted")
        exped = sem("exped")
        summing = sem("summing")
        inverted = sem("inverted")
        normed = sem("normed")
        turned = sem("turned")
        p_main = sem("p_main")
        p_rest = sem("p_rest")
        valued = sem("valued")
        owned = sem("owned")
        att_ready = sem("att_ready")
        wo_done = sem("wo_done")
        x1_ready = sem("x1_ready")
        x2_ready = sem("x2_ready")
        x2_main = sem("x2_main")
        x2_rest = sem("x2_rest")
        ft_done = sem("ft_done")
        ft_out = sem("ft_out")
        ff_done = sem("ff_done")
        ff_out = sem("ff_out")
        ffb_ready = sem("ffb_ready")
        out_ready = sem("out_ready")

        N_LOADS = 2 * (2 + 2 + 4) + 6 + 2 * NB + 1 + KC + 3

        def x_row(at, view):
            if isinstance(at.i, int):
                return view[2 * at.i + at.k]
            return view[bass.ds(at.i * 2 + at.k, 1), :, :, :].rearrange("n p q t -> (n p) q t")

        def bank_of_probs(k):
            return probs[:, k // 2, :, k % 2:NB:2, :]

        def half_of_blocks(tile, part):
            n = NU // 2 * KB
            return tile.rearrange("p (f c) -> p f c", f=2)[:, :, part * n:(part + 1) * n]

        block = es.enter_context(nc.Block())

        @block.sync
        def _(sp):
            def load(at):
                if at.k > 0:
                    sp.wait_ge(xn_ready, at.before(2))
                sp.dma_start(x_sb[:, :, :], x_row(at, x_v)).then_inc(x_in, 16)
                if at.k > 0:
                    sp.wait_ge(k_done, at.before(2))
                    sp.wait_ge(v_done, at.before(2))
                sp.dma_start(c_sb[:, :, :], x_row(at, ctx_v)).then_inc(c_in, 16)

            def load_residual(at):
                sp.wait_ge(x1_ready, at.before(2))
                sp.dma_start(xr_sb[:, :, :], x_row(at, x_v)).then_inc(xr_in, 16)

            def store(at):
                for pr in range(PAIRS):
                    sp.wait_ge(out_ready, at.after(2, pr))
                    sp.dma_start(x_row(at, out_v)[:, pr, :], x1[:, pr, :]).then_inc(stored[pr], 16)

            load(Step(0, 0))
            sp.wait_ge(setup_zeroed, 4)
            for b in range(2):
                r = slice(b * C, (b + 1) * C)
                sp.dma_start(wq_in[r, r], wq).then_inc(setup_loaded, 16)
                sp.dma_start(wk_in[r, r], wk).then_inc(setup_loaded, 16)
                for half in range(2):
                    rows = slice(half * 64 + b * 32, half * 64 + b * 32 + 32)
                    sp.dma_start(wv_in[rows, r], wv[half * 32:half * 32 + 32, :]).then_inc(setup_loaded, 16)
                    for pr in range(PAIRS):
                        cols = slice((2 * pr + b) * 32, (2 * pr + b) * 32 + 32)
                        sp.dma_start(wo_in[r, 2 * pr + half, cols],
                                     wo[:, half * 32:half * 32 + 32]).then_inc(setup_loaded, 16)
            for b in range(2):
                r = slice(b * C, (b + 1) * C)
                sp.dma_start(bq_sb[r, :], bq.unsqueeze(1)).then_inc(setup_loaded, 16)
                sp.dma_start(bk_sb[r, :], bk.unsqueeze(1)).then_inc(setup_loaded, 16)
                sp.dma_start(bo_sb[r, :], bo.unsqueeze(1)).then_inc(setup_loaded, 16)
            for b in range(NB):
                for half in range(2):
                    sp.dma_start(bv_sb[b * 32:b * 32 + 32, half:half + 1],
                                 bv[half * 32:half * 32 + 32].unsqueeze(1)).then_inc(setup_loaded, 16)
            sp.dma_start(bias_sb[:, :], bias.unsqueeze(0).broadcast_to([P, OUT_F])).then_inc(setup_loaded, 16)
            for c in range(KC):
                words = qweight[c * 16:(c + 1) * 16, :].unsqueeze(1).broadcast_to([16, NIB, OUT_F])
                sp.dma_start(word_i[:, c * OUT_F:(c + 1) * OUT_F], words).then_inc(setup_loaded, 16)
            sp.dma_start(z_in[0:GROUPS, :], qzeros).then_inc(setup_loaded, 16)
            sp.dma_start(s_h[0:GROUPS, :], scales).then_inc(setup_loaded, 16)
            sp.dma_start(g_i[0:GROUPS, :], g_idx.unsqueeze(0).broadcast_to([GROUPS, IN_F])).then_inc(setup_loaded, 16)
            load(Step(0, 1))
            load(Step(0, 2))
            load_residual(Step(0, 0))
            with sp.Fori(0, (STEPS - 4) // 2) as i:
                for k in (3, 4):
                    load(Step(i, k))
                    load_residual(Step(i, k - 2))
                    store(Step(i, k - 3))
            load(Step(0, STEPS - 1))
            load_residual(Step(0, STEPS - 3))
            store(Step(0, STEPS - 4))
            load_residual(Step(0, STEPS - 2))
            store(Step(0, STEPS - 3))
            load_residual(Step(0, STEPS - 1))
            store(Step(0, STEPS - 2))
            store(Step(0, STEPS - 1))
            for pr in range(PAIRS):
                sp.wait_ge(stored[pr], 16 * STEPS)

        @block.gpsimd
        def _(pool):
            for tile in (wq_in, wk_in, wv_in):
                pool.memset(tile[:, :], 0.0).then_inc(setup_zeroed, 1)
            pool.memset(wo_in[:, :, :], 0.0).then_inc(setup_zeroed, 1)
            pool.iota(part_i[:, 0:1], pattern=[[0, 1]], base=0, channel_multiplier=1).then_inc(iotas, 1)
            pool.iota(col_i[:, :], pattern=[[1, P]], base=0, channel_multiplier=0).then_inc(iotas, 1)
            pool.iota(t_i[:, :], pattern=[[0, H], [1, QB]], base=0, channel_multiplier=0).then_inc(iotas, 1)

            pool.memset(minus_half[:, :], -0.5).then_inc(half_ready, 1)
            pool.memset(eps[:, :], EPS).then_inc(half_ready, 1)
            pool.wait_ge(half_ready, 2)

            def root(at, mv, var_done, rs, rs_done):
                pool.wait_ge(var_done, at.after(2, 1))
                pool.tensor_tensor(rs[:, :], mv[:, :, 1], eps[:, :], ALU.add).then_inc(rs_done, 1)
                pool.wait_ge(rs_done, at.after(2, 0))
                pool.tensor_tensor(rs[:, :], rs[:, :], minus_half[:, :], ALU.pow).then_inc(rs_done, 1)

            def rest_of_pair(at, pr):
                pool.wait_ge(q_out, at.after(2, pr))
                if pr == 0:
                    pool.wait_ge(q_diag_ready, at.before(2))
                pool.tensor_tensor(q_parts[:, 1, pr, :], q32[:, :], q_parts[:, 0, pr, :],
                                   ALU.subtract).then_inc(q_rest, 1)
                pool.wait_ge(k_out, at.after(2, pr))
                real = slice(LEFT, LEFT + T)
                pool.tensor_tensor(k_parts[at.par][:, 1, pr, real], k32[:, :],
                                   k_parts[at.par][:, 0, pr, real], ALU.subtract).then_inc(k_rest, 1)

            def rest_of_v(at, part):
                pool.wait_ge(v_main, at.after(2, part))
                pool.tensor_tensor(half_of_blocks(v_parts[:, 1, :], part), half_of_blocks(vt32[:, :], part),
                                   half_of_blocks(v_parts[:, 0, :], part), ALU.subtract).then_inc(v_rest, 1)

            def sum_rows(at, k):
                pool.wait_ge(exped, at.after(8, k))
                src, width, lo = bank_of_probs(k), KB // 2, 0
                for level in range(LEVELS):
                    a, b = src[..., 0:width], src[..., width:2 * width]
                    if level:
                        pool.wait_ge(summing, at.after(8 * LEVELS, LEVELS * k + level - 1))
                    if level == LEVELS - 1:
                        if at.k > 0 or k >= 2:
                            pool.wait_ge(inverted, at.before(8) + k - 1)
                        dst = row_sum[:, k % 2, :].unsqueeze(2)
                    else:
                        dst = tree[:, :, lo:lo + width]
                        src = dst
                    if level == 0:
                        dst = dst.rearrange("p (u q) w -> p u q w", q=PAIRS)
                    pool.tensor_tensor(dst, a, b, ALU.add).then_inc(summing, 1)
                    lo += width
                    width //= 2

            def normalise(at, k):
                pool.wait_ge(inverted, at.after(8, k))
                src = bank_of_probs(k)
                inv = inv_sum[:, k % 2, :].rearrange("p (u q) -> p u q", q=PAIRS)
                pool.tensor_tensor(src, src, inv.unsqueeze(3).broadcast_to([P, OCT, PAIRS, KB]),
                                   ALU.mult).then_inc(normed, 1)

            def step(at, done2, done, cur, nxt):
                for s in range(SLOTS):
                    if nxt and s == 1:
                        root(at.shift(1), mean_var, x_var, rstd, x_rstd)
                    if done and s == 7:
                        root(at.shift(-1), mean_var2, x1_var, rstd2, x1_rstd)
                    for st, k in lagged(s, SUM_LAG, cur, done, at):
                        sum_rows(st, k)
                    for st, k in lagged(s, NORM_LAG, cur, done, at):
                        normalise(st, k)
                    if cur and s in (0, 5):
                        rest_of_v(at, s // 5)
                    if nxt and s in (3, 4):
                        rest_of_pair(at.shift(1), s - 3)

            root(Step(0, 0), mean_var, x_var, rstd, x_rstd)
            rest_of_pair(Step(0, 0), 0)
            rest_of_pair(Step(0, 0), 1)
            run_steps(pool, step)

        @block.scalar
        def _(act):
            act.wait_ge(setup_loaded, 16 * N_LOADS)

            def q_and_k_out(at, pr):
                act.wait_ge(q_done, at.after(2, pr))
                if not (at.k == 0 and pr == 0):
                    act.wait_ge(q_rest, at.before(2) + pr)
                if at.k > 0 and pr == 0:
                    act.wait_ge(q_diag_ready, at.before(2))
                act.activation(q32[:, :], ps_m[0][:, :], ACT.Identity, bias=bq_sb[:, 0:1])
                act.activation(q_parts[:, 0, pr, :], ps_m[0][:, :], ACT.Identity,
                               bias=bq_sb[:, 0:1]).then_inc(q_out, 1)
                act.wait_ge(k_done, at.after(2, pr))
                if not (at.k == 0 and pr == 0):
                    act.wait_ge(k_rest, at.before(2) + pr)
                act.activation(k32[:, :], ps_m[1][:, :], ACT.Identity, bias=bk_sb[:, 0:1])
                act.activation(k_parts[at.par][:, 0, pr, LEFT:LEFT + T], ps_m[1][:, :], ACT.Identity,
                               bias=bk_sb[:, 0:1]).then_inc(k_out, 1)

            def v_half_out(at, half):
                act.wait_ge(v_done, at.after(2, half))
                act.wait_ge(vt_ready, at.before(2))
                act.activation(v32[:, half, LEFT:LEFT + T], ps_m[half][:, :], ACT.Identity,
                               bias=bv_sb[:, half:half + 1]).then_inc(v_out, 1)

            def main_of_v(at, part):
                if part == 0:
                    act.wait_ge(vt_ready, at.after(2, 1))
                if at.k > 0:
                    act.wait_ge(v_diag_ready, at.shift(-1).after(2, part))
                act.activation(half_of_blocks(v_parts[:, 0, :], part), half_of_blocks(vt32[:, :], part),
                               ACT.Copy).then_inc(v_main, 1)

            def exp_bank(at, k):
                act.wait_ge(shifted, at.after(8, k))
                if at.k > 0:
                    act.wait_ge(turned, at.shift(-1).after(8, 2 * (k // 2) + 1))
                act.activation(bank_of_probs(k),
                               ps_s[k % S_BANKS][:, :].rearrange("p (u q w) -> p u q w", q=PAIRS, w=KB),
                               ACT.Exp, scale=float(HD) ** -0.5).then_inc(exped, 1)

            def main_of_probs(at, q):
                act.wait_ge(turned, at.after(8, q))
                if at.k > 0 or q >= 2:
                    act.wait_ge(valued, at.before(8) + q - 1)
                act.activation(pt[:, q % 2, 0, :, :],
                               ps_t[q % 2][:, :].rearrange("p (u c) -> p u c", c=P), ACT.Copy).then_inc(p_main, 1)

            def main_of_x2(at, pr):
                act.wait_ge(x2_ready, at.after(2, pr))
                if at.k > 0:
                    act.wait_ge(ft_done, at.shift(-1).after(2, pr))
                act.activation(x2_parts[:, pr, 0, :], x2[:, pr, :], ACT.Copy).then_inc(x2_main, 1)

            def x2_turned_out(at, pr):
                act.wait_ge(ft_done, at.after(2, pr))
                if at.k > 0:
                    act.wait_ge(ff_done, at.shift(-1).after(2, pr))
                act.activation(x2t[:, pr, :], ps_m[pr][:, :].bitcast(F16), ACT.Copy).then_inc(ft_out, 1)

            def ffn_out(at, pr):
                act.wait_ge(ff_done, at.after(2, pr))
                if at.k > 0:
                    act.wait_ge(ffb_ready, at.shift(-1).after(2, pr))
                act.activation(ff16[:, pr, :], ps_m[pr][:, :], ACT.Copy).then_inc(ff_out, 1)

            def step(at, done2, done, cur, nxt):
                for s in range(SLOTS):
                    if cur and s in (0, 2):
                        main_of_v(at, s // 2)
                    if done2 and s in (1, 2):
                        for pr in range(PAIRS):
                            (x2_turned_out if s == 1 else ffn_out)(at.shift(-2), pr)
                    if nxt and s in (3, 4):
                        q_and_k_out(at.shift(1), s - 3)
                    if nxt and s == 5:
                        v_half_out(at.shift(1), 0)
                        v_half_out(at.shift(1), 1)
                    if cur:
                        exp_bank(at, s)
                    for st, q in lagged(s, TURN_LAG, cur, done, at):
                        main_of_probs(st, q)
                    if done and s == 7:
                        main_of_x2(at.shift(-1), 0)
                        main_of_x2(at.shift(-1), 1)

            q_and_k_out(Step(0, 0), 0)
            q_and_k_out(Step(0, 0), 1)
            v_half_out(Step(0, 0), 0)
            v_half_out(Step(0, 0), 1)
            run_steps(act, step)

        @block.vector
        def _(dve):
            done = [0]

            def in_order(instruction):
                done[0] += 1
                instruction.then_inc(consts, 1)
                dve.wait_ge(consts, done[0])

            for par in range(2):
                in_order(dve.memset(k_parts[par][:, :, :, :], 0.0))
            in_order(dve.memset(v32[:, :, :], 0.0))
            dve.wait_ge(iotas, 3)
            in_order(dve.tensor_scalar(part_i[:, 1:2], part_i[:, 0:1], 63, None, ALU.bitwise_and))
            in_order(dve.tensor_scalar(part_i[:, 2:3], part_i[:, 1:2], 3, None, ALU.logical_shift_right))
            in_order(dve.tensor_scalar(part_i[:, 3:4], part_i[:, 0:1], 5, None, ALU.logical_shift_right))
            in_order(dve.tensor_scalar(shift_i[:, 0:1], part_i[:, 0:1], 7, 2, ALU.bitwise_and,
                                       ALU.logical_shift_left))
            in_order(dve.tensor_scalar(shift_i[:, 1:2], part_i[:, 0:1], 31, 3, ALU.bitwise_and,
                                       ALU.logical_shift_right))
            in_order(dve.tensor_copy(part_f[:, :], part_i[:, :]))
            in_order(dve.tensor_copy(col_f[:, :], col_i[:, :]))
            in_order(dve.tensor_copy(t_f[:, :], t_i[:, :]))
            in_order(dve.tensor_scalar(ident[:, :], col_f[:, :], part_f[:, 0:1], None, ALU.is_equal))
            in_order(dve.tensor_scalar(minus_ident[:, :], ident[:, :], -1.0, None, ALU.mult))
            in_order(dve.tensor_copy(ident16[:, :], ident[:, :]))
            in_order(dve.tensor_scalar(row_pick[:, :], t_f[:, :], part_f[:, 1:2], None, ALU.is_equal))
            in_order(dve.tensor_scalar(head_of_row[:, :], col_f[:, 0:H], part_f[:, 2:3], None, ALU.is_equal))
            in_order(dve.tensor_scalar(batch_of_row[:, :], col_f[:, 0:NB], part_f[:, 3:4], None, ALU.is_equal))
            in_order(dve.tensor_scalar(t_f[:, 0:KB], col_f[:, 0:KB], part_f[:, 1:2], None, ALU.subtract))
            in_order(dve.tensor_scalar(lo_f[:, :], t_f[:, 0:KB], 0.0, MASKED, ALU.is_lt, ALU.mult))
            in_order(dve.tensor_scalar(hi_f[:, :], t_f[:, 0:KB], float(WIN - 1), MASKED, ALU.is_gt, ALU.mult))
            in_order(dve.tensor_tensor(lo_f[:, :], lo_f[:, :], hi_f[:, :], ALU.add))
            in_order(dve.tensor_copy(window[:, :, :], lo_f[:, :].unsqueeze(1).broadcast_to([P, 16, KB])))
            in_order(dve.tensor_copy(part_f[:, 0:1], shift_i[:, 1:2]))
            in_order(dve.tensor_scalar(head_of_col[:, :], col_f[:, 0:4], part_f[:, 0:1], None, ALU.is_equal))

            dve.wait_ge(setup_loaded, 16 * N_LOADS)
            in_order(dve.tensor_copy(part_f[:, 0:1], part_i[:, 0:1]))
            zi = z_i[0:GROUPS, :].rearrange("g (w j) -> g w j", j=NIB)
            for j in range(NIB):
                in_order(dve.tensor_scalar(zi[:, :, j], z_in[0:GROUPS, :], 4 * j, 15,
                                           ALU.logical_shift_right, ALU.bitwise_and))
            in_order(dve.tensor_copy(z_h[0:GROUPS, :], z_i[0:GROUPS, :]))
            g, neg = g_f[0:GROUPS, :], gneg_f[0:GROUPS, :]
            in_order(dve.tensor_copy(g, g_i[0:GROUPS, :]))
            in_order(dve.tensor_scalar(neg, g, 0.0, float(GROUPS), ALU.is_lt, ALU.mult))
            in_order(dve.tensor_tensor(g, g, neg, ALU.add))
            in_order(dve.tensor_scalar(g, g, 0.0, float(GROUPS - 1), ALU.max, ALU.min))
            in_order(dve.tensor_scalar(hot_h[0:GROUPS, :], g, part_f[0:GROUPS, 0:1], None, ALU.is_equal))
            hot_at = done[0]
            in_order(dve.tensor_tensor(nib_i[:, :], word_i[:, :],
                                       shift_i[:, 0:1].broadcast_to([P, KC * OUT_F]),
                                       ALU.logical_shift_right))
            in_order(dve.tensor_scalar(nib_i[:, :], nib_i[:, :], 15, None, ALU.bitwise_and))
            in_order(dve.tensor_copy(nib_f[:, :], nib_i[:, :]))
            for c in range(KC):
                cols = slice(c * OUT_F, (c + 1) * OUT_F)
                dve.wait_ge(setup_pe, 2 * c + 1)
                in_order(dve.tensor_tensor(lev_h[:, cols], nib_f[:, cols], ps_t[0][:, :], ALU.subtract))
                dve.wait_ge(setup_pe, 2 * c + 2)
                in_order(dve.tensor_tensor(w_ffn[:, c, :], lev_h[:, cols], ps_t[1][:, :], ALU.mult))
            dve.wait_ge(setup_pe, 2 * KC + 1)
            for n, tile in enumerate((wq_t, wk_t, wv_t)):
                dve.tensor_copy(tile[:, :], ps_m[0][:, n * P:(n + 1) * P]).then_inc(wt_copied, 1)
            dve.wait_ge(setup_pe, 2 * KC + 2)
            dve.tensor_copy(wo_t[:, :, :], ps_m[1][:, :].rearrange("p (n c) -> p n c", c=P)).then_inc(wt_copied, 1)
            assert hot_at == HOT_AT, hot_at

            def moments(at, src, st, stats_done, mv, var_done):
                for pr in range(PAIRS):
                    dve.bn_stats(st[:, pr, :], src[:, pr, :]).then_inc(stats_done, 1)
                dve.wait_ge(stats_done, at.after(2, 1))
                dve.memset(gate[:, :], 0.0)
                for pr in range(PAIRS):
                    dve.bn_aggr(mv[:, pr, :], st[:, pr, :]).then_inc(var_done, 1)

            def normed_rows(at, src, dst, mv, rs, ready):
                for pr in range(PAIRS):
                    dve.tensor_scalar(dst[:, pr, :], src[:, pr, :], mv[:, pr, 0:1], rs[:, pr:pr + 1],
                                      ALU.subtract, ALU.mult).then_inc(ready, 1)

            def moments_x(at):
                dve.wait_ge(x_in, at.before(16) + 16)
                moments(at, x_sb, stats, x_stats, mean_var, x_var)

            def norm_x(at):
                dve.wait_ge(x_rstd, at.after(2, 1))
                dve.wait_ge(q_done, at.before(2))
                normed_rows(at, x_sb, xn, mean_var, rstd, xn_ready)

            def q_diagonals(at, pr):
                dve.wait_ge(q_rest, at.after(2, pr))
                if at.k >= 2 and pr == 0:
                    dve.wait_ge(scored, at.shift(-1).before(8))
                src = q_parts[:, :, pr, :].rearrange("p a (u t) -> p a u t", t=QB)
                dst = q_diag[at.par][:, :, :, :].rearrange("p (a q u) h t -> p a q u h t", a=2, q=PAIRS)
                for h in range(H):
                    op = dve.tensor_scalar(dst[:, :, pr, :, h, :], src, head_of_row[:, h:h + 1], None, ALU.mult)
                op.then_inc(q_diag_ready, 1)

            def turn_v(at, half):
                dve.wait_ge(v_out, at.after(2, half))
                if half == 0:
                    dve.wait_ge(v_rest, at.before(2))
                keys = v32[:, half, :]
                src = bass.AP(keys.tensor, keys.offset, [keys.ap[0], [QB, NU], [1, KB]])
                dst = vt32[:, half * NU * KB:(half + 1) * NU * KB].rearrange("p (u c) -> p u c", c=KB)
                dve.transpose(dst, src).then_inc(vt_ready, 1)

            def v_diagonals(at, part, batches):
                if batches[0] == 0:
                    dve.wait_ge(v_rest, at.after(2, part))
                    dve.wait_ge(valued, at.before(8) - (4 if part == 0 and at.k else 0))
                blocks = slice(part * NU // 2, (part + 1) * NU // 2)
                src = v_parts[:, :, :].rearrange("p a (f u c) -> p (a f) u c", f=2, c=KB)[:, :, blocks, :]
                for b in batches:
                    op = dve.tensor_scalar(v_diag[:, :, blocks, b, :], src, batch_of_row[:, b:b + 1], None, ALU.mult)
                if batches[-1] == NB - 1:
                    op.then_inc(v_diag_ready, 1)

            def maxima(at, k):
                dve.wait_ge(scored, at.after(8, k))
                dve.tensor_reduce(row_max[:, k % S_BANKS, :],
                                  ps_s[k % S_BANKS][:, :].rearrange("p (c w) -> p c w", w=KB),
                                  AX.X, ALU.max).then_inc(maxed, 1)

            def invert(at, k):
                dve.wait_ge(summing, at.after(8 * LEVELS, LEVELS * k + LEVELS - 1))
                if at.k > 0 or k >= 2:
                    dve.wait_ge(normed, at.before(8) + k - 1)
                dve.reciprocal(inv_sum[:, k % 2, :], row_sum[:, k % 2, :]).then_inc(inverted, 1)

            def rest_of_probs(at, q):
                dve.wait_ge(p_main, at.after(8, q))
                dve.tensor_tensor(pt[:, q % 2, 1, :, :], ps_t[q % 2][:, :].rearrange("p (u c) -> p u c", c=P),
                                  pt[:, q % 2, 0, :, :], ALU.subtract).then_inc(p_rest, 1)

            def own_heads(at, q):
                dve.wait_ge(valued, at.after(8, q))
                if at.k > 0 or q > 0:
                    dve.wait_ge(att_ready, at.before(8) + q)
                mask = head_of_col[:, :].unsqueeze(1).unsqueeze(3).broadcast_to([P, 8, 4, QB])
                dve.tensor_tensor(own[:, :].rearrange("p (a h t) -> p a h t", h=4, t=QB),
                                  ps_o[:, :].rearrange("p (a h t) -> p a h t", h=4, t=QB),
                                  mask, ALU.mult).then_inc(owned, 1)
                dve.wait_ge(owned, at.after(8, q))
                if q == 0:
                    dve.wait_ge(wo_done, at.before(2))
                dve.tensor_reduce(att[:, q, :, :].rearrange("p f (u t) -> p (f u) t", t=QB),
                                  own[:, :].rearrange("p (a h t) -> p a t h", h=4, t=QB),
                                  AX.X, ALU.add).then_inc(att_ready, 1)

            def residual(at):
                dve.wait_ge(xr_in, at.before(16) + 16)
                for pr in range(PAIRS):
                    dve.wait_ge(wo_done, at.after(2, pr))
                    dve.wait_ge(stored[pr], at.before(16))
                    dve.scalar_tensor_tensor(x1[:, pr, :], ps_m[pr][:, :], bo_sb[:, 0:1], xr_sb[:, pr, :],
                                             ALU.add, ALU.add).then_inc(x1_ready, 1)

            def moments_x1(at):
                dve.wait_ge(x1_ready, at.after(2, 1))
                moments(at, x1, stats2, x1_stats, mean_var2, x1_var)

            def norm_x1(at):
                dve.wait_ge(x1_rstd, at.after(2, 1))
                normed_rows(at, x1, x2, mean_var2, rstd2, x2_ready)

            def rest_of_x2(at, pr):
                dve.wait_ge(x2_main, at.after(2, pr))
                dve.wait_ge(x2_ready, at.after(2, pr))
                dve.tensor_tensor(x2_parts[:, pr, 1, :], x2[:, pr, :], x2_parts[:, pr, 0, :],
                                  ALU.subtract).then_inc(x2_rest, 1)

            def outputs(at, pr):
                dve.wait_ge(ff_out, at.after(2, pr))
                dve.wait_ge(out_ready, at.before(2) + pr)
                dve.tensor_tensor(ffb[:, :], ff16[:, pr, :], bias_sb[:, :], ALU.add).then_inc(ffb_ready, 1)
                dve.wait_ge(ffb_ready, at.after(2, pr))
                dve.tensor_tensor(x1[:, pr, :], x1[:, pr, :], ffb[:, :], ALU.add).then_inc(out_ready, 1)

            def step(at, done2, done, cur, nxt):
                for s in range(SLOTS):
                    if cur:
                        maxima(at, s)
                    for st, q in lagged(s, REST_LAG, cur, done, at):
                        rest_of_probs(st, q)
                    for st, q in lagged(s, VALUE_LAG, cur, done, at):
                        own_heads(st, q)
                    for st, k in lagged(s, SUM_LAG, cur, done, at):
                        invert(st, k)
                    if nxt and s == 0:
                        moments_x(at.shift(1))
                    if done2 and s == 0:
                        rest_of_x2(at.shift(-2), 0)
                        rest_of_x2(at.shift(-2), 1)
                    if nxt and s == 1:
                        norm_x(at.shift(1))
                    if done and s in (0, 1):
                        v_diagonals(at.shift(-1), 1, (range(0, 1), range(1, NB))[s])
                    if cur and s in (2, 3):
                        v_diagonals(at, 0, (range(0, 2), range(2, NB))[s - 2])
                    if done2 and s in (2, 3):
                        outputs(at.shift(-2), s - 2)
                    if nxt and s in (4, 5):
                        q_diagonals(at.shift(1), s - 4)
                    if done and s == 6:
                        residual(at.shift(-1))
                        moments_x1(at.shift(-1))
                    if done and s == 7:
                        norm_x1(at.shift(-1))
                    if nxt and s == 7:
                        turn_v(at.shift(1), 0)
                        turn_v(at.shift(1), 1)

            first = Step(0, 0)
            moments_x(first)
            norm_x(first)
            q_diagonals(first, 0)
            q_diagonals(first, 1)
            turn_v(first, 0)
            turn_v(first, 1)
            run_steps(dve, step)

        @block.tensor
        def _(pe):
            pe.wait_ge(consts, HOT_AT)
            for c in range(KC):
                hot = hot_h[0:GROUPS, c * P:(c + 1) * P]
                if c:
                    pe.wait_ge(consts, HOT_AT + 3 + 2 * (c - 1) + 1)
                pe.matmul(ps_t[0][:, :], hot, z_h[0:GROUPS, :], start=True, stop=True).then_inc(setup_pe, 1)
                if c:
                    pe.wait_ge(consts, HOT_AT + 3 + 2 * (c - 1) + 2)
                pe.matmul(ps_t[1][:, :], hot, s_h[0:GROUPS, :], start=True, stop=True).then_inc(setup_pe, 1)
            pe.wait_ge(setup_loaded, 16 * N_LOADS)
            for n, tile in enumerate((wq_in, wk_in, wv_in)):
                last = pe.transpose(ps_m[0][:, n * P:(n + 1) * P], tile[:, :], ident[:, :])
            last.then_inc(setup_pe, 1)
            for n in range(4):
                last = pe.transpose(ps_m[1][:, n * P:(n + 1) * P], wo_in[:, n, :], ident[:, :])
            last.then_inc(setup_pe, 1)
            pe.wait_ge(wt_copied, 4)

            def project_q_k(at, pr):
                pe.wait_ge(xn_ready, at.after(2, pr))
                if pr == 0 and at.k > 0:
                    pe.wait_ge(v_out, at.before(2))
                    if at.k > 2:
                        pe.wait_ge(ff_out, at.shift(-2).before(2))
                if pr == 1:
                    pe.wait_ge(q_out, at.after(2, 0))
                pe.matmul(ps_m[0][:, :], wq_t[:, :], xn[:, pr, :], start=True, stop=True).then_inc(q_done, 1)
                if pr == 0:
                    pe.wait_ge(c_in, at.before(16) + 16)
                if pr == 1:
                    pe.wait_ge(k_out, at.after(2, 0))
                pe.matmul(ps_m[1][:, :], wk_t[:, :], c_sb[:, pr, :],
                          start=True, stop=True).then_inc(k_done, 1)

            def project_v(at, half):
                pe.wait_ge(k_out if half else q_out, at.after(2, 1))
                for pr in range(PAIRS):
                    last = pe.matmul(ps_m[half][pr * 64:pr * 64 + 64, :], wv_t[:, half * 64:half * 64 + 64],
                                     c_sb[:, pr, :], start=True, stop=True)
                last.then_inc(v_done, 1)

            def scores(at, k):
                octet, side = k // 2, k % 2
                bank = ps_s[k % S_BANKS]
                if k == 0:
                    pe.wait_ge(q_diag_ready, at.after(2, 1))
                    pe.wait_ge(k_rest, at.after(2, 1))
                if k >= S_BANKS:
                    pe.wait_ge(exped, at.after(8, k - S_BANKS))
                elif at.k > 0:
                    pe.wait_ge(exped, at.shift(-1).after(8, LAST_ON_BANK[k]))
                rows = slice(side * 64, side * 64 + 64)
                pe.matmul(bank[:, :], row_pick[rows, :],
                          window[rows, :, :].rearrange("p c w -> p (c w)"),
                          start=True, stop=False, skip_group_check=True)
                for u in range(OCT):
                    for pr in range(PAIRS):
                        blk = octet * OCT + u
                        cell = (u * PAIRS + pr) * KB
                        for qp, kp in ((0, 0), (0, 1), (1, 0)):
                            last = pe.matmul(bank[:, cell:cell + KB],
                                             q_diag[at.par][rows, (qp * PAIRS + pr) * NU + blk, :, :]
                                             .rearrange("p h t -> p (h t)"),
                                             k_parts[at.par][rows, kp, pr, blk * QB:blk * QB + KB],
                                             start=False, stop=False, skip_group_check=True)
                last.then_inc(scored, 1)

            def shift_scores(at, k):
                pe.wait_ge(maxed, at.after(8, k))
                pe.matmul(ps_s[k % S_BANKS][:, :].rearrange("p (c w) -> p c w", w=KB), minus_ident[:, :],
                          row_max[:, k % S_BANKS, :].unsqueeze(2).broadcast_to([P, 16, KB]),
                          start=False, stop=True, skip_group_check=True).then_inc(shifted, 1)

            def turn_probs(at, q):
                pe.wait_ge(normed, at.after(8, 2 * (q // 2) + 1))
                if at.k > 0 or q >= 2:
                    pe.wait_ge(p_rest, at.before(8) + q - 1)
                for j in range(4):
                    last = pe.transpose(ps_t[q % 2][:, j * P:(j + 1) * P],
                                        probs[:, q // 2, 4 * (q % 2) + j, :, :].rearrange("p b w -> p (b w)"),
                                        ident[:, :])
                last.then_inc(turned, 1)

            def values(at, q):
                if q in (0, NQ // 2):
                    pe.wait_ge(v_diag_ready, at.after(2, q // (NQ // 2)))
                pe.wait_ge(p_rest, at.after(8, q))
                if at.k > 0 or q > 0:
                    pe.wait_ge(owned, at.before(8) + q)
                for half in range(2):
                    for j in range(4):
                        cell = (half * 4 + j) * 64
                        terms = ((0, 0), (0, 1), (1, 0))
                        for n, (vp, pp) in enumerate(terms):
                            last = pe.matmul(ps_o[:, cell:cell + 64],
                                             v_diag[:, vp * 2 + half, 4 * q + j, :, :]
                                             .rearrange("p b c -> p (b c)"),
                                             pt[:, q % 2, pp, j, half * 64:half * 64 + 64],
                                             start=n == 0, stop=n == len(terms) - 1)
                last.then_inc(valued, 1)

            def project_out(at, nxt):
                pe.wait_ge(att_ready, at.after(8, NQ - 1))
                if nxt:
                    pe.wait_ge(v_out, at.shift(2).after(2, 1))
                else:
                    pe.wait_ge(ff_out, at.before(2))
                for pr in range(PAIRS):
                    for half in range(2):
                        last = pe.matmul(ps_m[pr][:, :], wo_t[:, 2 * pr + half, :],
                                         att[:, :, half, :], start=half == 0, stop=half == 1)
                    last.then_inc(wo_done, 1)

            def turn_x2(at, pr):
                pe.wait_ge(x2_rest, at.after(2, pr))
                for part in range(2):
                    for c in range(KC):
                        n = part * KC + c
                        last = pe.transpose(ps_m[pr][:, :].bitcast(F16)[:, n * P:(n + 1) * P],
                                            x2_parts[:, pr, part, c * P:(c + 1) * P], ident16[:, :])
                last.then_inc(ft_done, 1)

            def feed_forward(at, pr):
                pe.wait_ge(ft_out, at.after(2, pr))
                for n in range(2 * KC):
                    last = pe.matmul(ps_m[pr][:, :], x2t[:, pr, n * P:(n + 1) * P], w_ffn[:, n % KC, :],
                                     start=n == 0, stop=n == 2 * KC - 1)
                last.then_inc(ff_done, 1)

            def step(at, done2, done, cur, nxt):
                for s in range(SLOTS):
                    for st, q in lagged(s, VALUE_LAG, cur, done, at):
                        values(st, q)
                    if cur:
                        shift_scores(at, s)
                    for st, q in lagged(s, TURN_LAG, cur, done, at):
                        turn_probs(st, q)
                    if cur and s < SLOTS - 1:
                        scores(at, s + 1)
                    if nxt and s == SLOTS - 1:
                        scores(at.shift(1), 0)
                    if done2 and s in (0, 1):
                        for pr in range(PAIRS):
                            (turn_x2 if s == 0 else feed_forward)(at.shift(-2), pr)
                    if nxt and s in (2, 3):
                        project_q_k(at.shift(1), s - 2)
                    if nxt and s == 4:
                        project_v(at.shift(1), 0)
                        project_v(at.shift(1), 1)
                    if done and s == 5:
                        project_out(at.shift(-1), nxt)

            first = Step(0, 0)
            project_q_k(first, 0)
            project_q_k(first, 1)
            project_v(first, 0)
            project_v(first, 1)
            scores(first, 0)
            run_steps(pe, step)


HOT_AT = 3 + 21 + 1 + NIB + 1 + 5

_INS = ['x', 'ctx_4096', 'L0_xattn_Wq', 'L0_xattn_bq', 'L0_xattn_Wk', 'L0_xattn_bk', 'L0_xattn_Wv', 'L0_xattn_bv',
        'L0_xattn_Wo', 'L0_xattn_bo', 'L0_ffn_qweight', 'L0_ffn_qzeros', 'L0_ffn_scales', 'L0_ffn_g_idx',
        'L0_ffn_bias']


def kernel(**inputs):
    import numpy as _np
    import concourse.bacc as _bacc
    from concourse import mybir as _mybir
    from concourse.bass_utils import run_bass_kernel_spmd as _run

    nc = _bacc.Bacc("TRN2", target_bir_lowering=False, num_devices=1)
    arrays, args = {}, []
    for name in _INS:
        a = _np.ascontiguousarray(inputs[name])
        arrays[f"in_{name}"] = a
        args.append(nc.dram_tensor(f"in_{name}", a.shape, _mybir.dt.from_np(a.dtype), kind="ExternalInput").ap())
    result = nc.dram_tensor("result", (B, C, T), F32, kind="ExternalOutput").ap()
    build(nc, *args, result)
    r = _run(nc, [arrays], core_ids=[0])
    return r.results[0]["result"]
```

```python
from contextlib import ExitStack

import concourse.bass as bass
from concourse import mybir

F32 = mybir.dt.float32
BF16 = mybir.dt.bfloat16
F16 = mybir.dt.float16
I32 = mybir.dt.int32
ALU = mybir.AluOpType
ACT = mybir.ActivationFunctionType
AX = mybir.AxisListType

P = 128
B, C, T = 32, 64, 512
H, WIN = 8, 16
HD = C // H
HH = H // 2
PAIRS = 2
NB = 2 * PAIRS
STEPS = B // NB
QB = 16
KB = 32
NU = T // QB
LEFT = WIN // 2
TP = (NU - 1) * QB + KB
OCT = 8
NQ = NU // 4
NO = NU // OCT
CELLS = OCT * NB
SLOTS = 8
GROUPS, IN_F, OUT_F = 4, 512, 512
NIB = 8
KC = IN_F // P
EPS = 1e-5
MASKED = -1e30
SUM_LAG, NORM_LAG = 2, 3
TURN_LAG, REST_LAG, VALUE_LAG = 4, 5, 6
S_BANKS = 3
LEVELS = 5
LAST_ON_BANK = {0: 6, 1: 7, 2: 5}


class Step:

    def __init__(self, i, k):
        self.i, self.k = i, k
        self.par = k % 2

    def after(self, per, event=0):
        return self.i * (2 * per) + (self.k * per + event + 1)

    def before(self, per):
        return self.i * (2 * per) + self.k * per

    def shift(self, d):
        return Step(self.i, self.k + d)


def run_steps(eng, step):
    step(Step(0, 0), False, False, True, True)
    step(Step(0, 1), False, True, True, True)
    with eng.Fori(0, (STEPS - 4) // 2) as i:
        step(Step(i, 2), True, True, True, True)
        step(Step(i, 3), True, True, True, True)
    step(Step(0, STEPS - 2), True, True, True, True)
    step(Step(0, STEPS - 1), True, True, True, False)
    step(Step(0, STEPS), True, True, False, False)
    step(Step(0, STEPS + 1), True, False, False, False)


def lagged(s, lag, cur, done, at):
    if s >= lag:
        return [(at, s - lag)] if cur else []
    return [(at.shift(-1), s - lag + SLOTS)] if done else []


def lagged_octet(s, lag, cur, done, at):
    return [(st, k // 2) for st, k in lagged(s, lag, cur, done, at) if k % 2 == 0]


def build(nc, x, ctx_in, wq, bq, wk, bk, wv, bv, wo, bo, qweight, qzeros, scales, g_idx, bias, out):
    x_v = x.rearrange("(n q b) c t -> n (b c) q t", q=PAIRS, b=2)
    ctx_v = ctx_in.rearrange("(n q b) c t -> n (b c) q t", q=PAIRS, b=2)
    out_v = out.rearrange("(n q b) c t -> n (b c) q t", q=PAIRS, b=2)

    with ExitStack() as es:
        def sb(name, shape, dt=F32):
            return es.enter_context(nc.sbuf_tensor(name, shape, dt))

        def ps(name):
            return es.enter_context(nc.psum_tensor(name, [P, 512], F32))

        def sem(name):
            return es.enter_context(nc.semaphore(name))

        x_sb = sb("x_sb", [P, PAIRS, T])
        c_sb = sb("c_sb", [P, PAIRS, T])
        stats = sb("stats", [P, PAIRS, 6])
        mean_var = sb("mean_var", [P, PAIRS, 2])
        rstd, shift, rstd2, shift2 = (sb(name, [P, PAIRS]) for name in ("rstd", "shift", "rstd2", "shift2"))
        xn = sb("xn", [P, PAIRS, T])
        q32 = sb("q32", [P, T])
        k32 = sb("k32", [P, T])
        q_parts = sb("q_parts", [P, 2, PAIRS, T], F16)
        k_parts = [sb(f"k_parts{i}", [P, 2, PAIRS, TP], F16) for i in range(2)]
        q_diag = [sb(f"q_diag{i}", [P, 2 * PAIRS * NU, H, QB], F16) for i in range(2)]
        v32 = sb("v32", [P, 2, TP])
        vt32 = sb("vt32", [P, 2 * NU * KB])
        v_parts = sb("v_parts", [P, 2, 2 * NU * KB], F16)
        v_diag = sb("v_diag", [P, 2 * 2, NU, HH, NB, HD], F16)
        row_max = sb("row_max", [P, S_BANKS, 16], BF16)
        probs = sb("probs", [P, NU // OCT, OCT, NB, KB])
        tree = sb("tree", [P, CELLS, KB // 2])
        row_sum = sb("row_sum", [P, 2, CELLS])
        inv_sum = sb("inv_sum", [P, 2, CELLS])
        pt = sb("pt", [P, 2, 2, 4, P], F16)
        att = [sb(f"att{i}", [P, NQ, 2, 64]) for i in range(2)]
        xr_sb = sb("xr_sb", [P, PAIRS, T])
        x1 = sb("x1", [P, PAIRS, T])
        stats2 = sb("stats2", [P, PAIRS, 6])
        mean_var2 = sb("mean_var2", [P, PAIRS, 2])
        minus_half = sb("minus_half", [P, PAIRS])
        gate = sb("gate", [P, 1])
        shift_i = sb("shift_i", [P, 1], I32)
        x2 = sb("x2", [P, PAIRS, T])
        x2_parts = sb("x2_parts", [P, PAIRS, 2, T], F16)
        x2t = sb("x2t", [P, PAIRS, 2 * KC * P], F16)
        ff16 = sb("ff16", [P, PAIRS, T], F16)

        wq_t = sb("wq_t", [P, P])
        wk_t = sb("wk_t", [P, P])
        wv_t = sb("wv_t", [P, P])
        wo_t = sb("wo_t", [P, 4, P])
        biases = sb("biases", [P, 5])
        bq_sb, bk_sb, bo_sb, bv_sb = biases[:, 0:1], biases[:, 1:2], biases[:, 2:3], biases[:, 3:5]
        bias_sb = sb("bias_sb", [P, OUT_F], F16)
        ident = sb("ident", [P, P])
        ident16 = sb("ident16", [P, P], F16)
        minus_ident = sb("minus_ident", [P, P], BF16)
        window = sb("window", [P, KB])
        head_of_row = sb("head_of_row", [P, H])
        batch_of_row = sb("batch_of_row", [P, NB])
        w_ffn = sb("w_ffn", [P, KC, OUT_F], F16)

        early = att[0][:, :, :, :].rearrange("p q f t -> p (q f t)")
        wq_in, wk_in, wv_in = (early[:, n * P:(n + 1) * P] for n in range(3))
        wo_in = early[:, 3 * P:7 * P].rearrange("p (n c) -> p n c", c=P)
        w_rows = ff16[:, :, :].rearrange("p q t -> p (q t)").bitcast(F32).rearrange("p (n c) -> p n c", c=C)

        scratch = v_diag[:, :, :, :, :, :].rearrange("p a u h b c -> p (a u h b c)")
        taken = [0]

        def carve(n, dt):
            taken[0] += 2 * n
            return scratch[:, taken[0] - 2 * n:taken[0]].bitcast(dt)

        part_i, part_f = carve(4, I32), carve(4, F32)
        col_i, col_f = carve(P, I32), carve(P, F32)
        ahead, before, beyond = carve(KB, F32), carve(KB, F32), carve(KB, F32)
        z_in, z_i = carve(OUT_F // NIB, I32), carve(OUT_F, I32)
        g_i, g_f, gneg_f = carve(IN_F, I32), carve(IN_F, F32), carve(IN_F, F32)
        words = [(x1, x2)[c // 2][:, c % 2, :].bitcast(I32) for c in range(KC)]
        lev_h, z_h, s_h, hot_h = (x2t[:, n // 2, (n % 2) * 512:(n % 2) * 512 + 512] for n in range(4))

        ps_s = [ps(f"ps_s{i}") for i in range(S_BANKS)]
        ps_t = [ps(f"ps_t{i}") for i in range(2)]
        ps_o = ps("ps_o")
        ps_m = [ps(f"ps_m{i}") for i in range(2)]

        weights_in = sem("weights_in")
        biases_in = sem("biases_in")
        ffn_in = sem("ffn_in")
        words_in = sem("words_in")
        zeroed = sem("zeroed")
        iotas = sem("iotas")
        ident_ready = sem("ident_ready")
        consts = sem("consts")
        consts_ready = sem("consts_ready")
        tables = sem("tables")
        tables_ready = sem("tables_ready")
        dequant = sem("dequant")
        spread = sem("spread")
        laid = sem("laid")
        w_turned = sem("w_turned")
        wt_copied = sem("wt_copied")
        x_in = sem("x_in")
        c_in = sem("c_in")
        xr_in = sem("xr_in")
        stored = [sem(f"stored{i}") for i in range(PAIRS)]
        half_ready = sem("half_ready")
        x_stats = sem("x_stats")
        x_var = sem("x_var")
        x_rstd = sem("x_rstd")
        x1_stats = sem("x1_stats")
        x1_var = sem("x1_var")
        x1_rstd = sem("x1_rstd")
        xn_ready = sem("xn_ready")
        q_done = sem("q_done")
        k_done = sem("k_done")
        v_done = sem("v_done")
        q_out = sem("q_out")
        k_out = sem("k_out")
        v_out = sem("v_out")
        q_rest = sem("q_rest")
        k_rest = sem("k_rest")
        q_diag_ready = sem("q_diag_ready")
        vt_ready = sem("vt_ready")
        v_main = sem("v_main")
        v_rest = sem("v_rest")
        v_diag_ready = sem("v_diag_ready")
        scored = sem("scored")
        maxed = sem("maxed")
        shifted = sem("shifted")
        exped = sem("exped")
        windowed = sem("windowed")
        summing = sem("summing")
        inverted = sem("inverted")
        normed = sem("normed")
        turned = sem("turned")
        p_main = sem("p_main")
        p_rest = sem("p_rest")
        valued = sem("valued")
        att_ready = sem("att_ready")
        wo_done = sem("wo_done")
        x1_ready = sem("x1_ready")
        x2_ready = sem("x2_ready")
        x2_main = sem("x2_main")
        x2_rest = sem("x2_rest")
        ft_done = sem("ft_done")
        ft_out = sem("ft_out")
        ff_done = sem("ff_done")
        ff_out = sem("ff_out")
        ff_biased = sem("ff_biased")
        out_ready = sem("out_ready")

        N_FFN_LOADS = 4

        def x_row(at, view):
            if isinstance(at.i, int):
                return view[2 * at.i + at.k]
            return view[bass.ds(at.i * 2 + at.k, 1), :, :, :].rearrange("n p q t -> (n p) q t")

        def bank_of_probs(k):
            return probs[:, k // 2, :, k % 2:NB:2, :]

        def half_of_blocks(tile, part):
            n = NU // 2 * KB
            return tile.rearrange("p (f c) -> p f c", f=2)[:, :, part * n:(part + 1) * n]

        def of_head(at, q, h):
            rows = slice(h * NB * HD, (h + 1) * NB * HD)
            return (att[at.par][rows, q, :, :].rearrange("p f (u t) -> p (f u) t", t=QB),
                    ps_o[rows, :].rearrange("p (a h t) -> p a h t", h=HH, t=QB)[:, :, h, :])

        block = es.enter_context(nc.Block())

        @block.sync
        def _(sp):
            def load_x(at):
                if at.k > 0:
                    sp.wait_ge(xn_ready, at.before(2))
                sp.dma_start(x_sb[:, :, :], x_row(at, x_v)).then_inc(x_in, 16)

            def load_c(at):
                if at.k > 0:
                    sp.wait_ge(k_done, at.before(2))
                    sp.wait_ge(v_done, at.before(2))
                sp.dma_start(c_sb[:, :, :], x_row(at, ctx_v)).then_inc(c_in, 16)

            def load(at):
                load_x(at)
                load_c(at)

            def load_residual(at):
                sp.wait_ge(x1_ready, at.before(2))
                sp.dma_start(xr_sb[:, :, :], x_row(at, x_v)).then_inc(xr_in, 16)

            def store(at):
                for pr in range(PAIRS):
                    sp.wait_ge(out_ready, at.after(2, pr))
                    sp.dma_start(x_row(at, out_v)[:, pr, :], x1[:, pr, :]).then_inc(stored[pr], 16)

            def twice(w):
                return w.unsqueeze(0).broadcast_to([2, C, w.shape[1]])

            load_x(Step(0, 0))
            sp.dma_start(w_rows[:, 0, :], twice(wq)).then_inc(weights_in, 16)
            sp.dma_start(w_rows[:, 1, :], twice(wk)).then_inc(weights_in, 16)
            for half in range(2):
                sp.dma_start(w_rows[half * 64:half * 64 + 64, 2, :],
                             wv[half * 32:half * 32 + 32, :].unsqueeze(0).broadcast_to([2, 32, C])
                             ).then_inc(weights_in, 16)
            sp.dma_start(w_rows[:, 3, :], twice(wo)).then_inc(weights_in, 16)
            load_c(Step(0, 0))
            for tile, vector in ((bq_sb, bq), (bk_sb, bk), (bo_sb, bo)):
                sp.dma_start(tile, twice(vector.unsqueeze(1))).then_inc(biases_in, 16)
            for half in range(2):
                sp.dma_start(bv_sb[:, half:half + 1], bv[half * 32:half * 32 + 32].unsqueeze(1).unsqueeze(0)
                             .broadcast_to([NB, 32, 1])).then_inc(biases_in, 16)
            sp.dma_start(z_in[0:GROUPS, :], qzeros).then_inc(ffn_in, 16)
            sp.dma_start(s_h[0:GROUPS, :], scales).then_inc(ffn_in, 16)
            sp.dma_start(g_i[0:GROUPS, :], g_idx.unsqueeze(0).broadcast_to([GROUPS, IN_F])).then_inc(ffn_in, 16)
            sp.dma_start(bias_sb[:, :], bias.unsqueeze(0).broadcast_to([P, OUT_F])).then_inc(ffn_in, 16)
            for c in range(KC):
                rows = qweight[c * 16:(c + 1) * 16, :].unsqueeze(1).broadcast_to([16, NIB, OUT_F])
                sp.dma_start(words[c], rows).then_inc(words_in, 16)
            load(Step(0, 1))
            load(Step(0, 2))
            load_residual(Step(0, 0))
            with sp.Fori(0, (STEPS - 4) // 2) as i:
                for k in (3, 4):
                    load(Step(i, k))
                    load_residual(Step(i, k - 2))
                    store(Step(i, k - 3))
            load(Step(0, STEPS - 1))
            load_residual(Step(0, STEPS - 3))
            store(Step(0, STEPS - 4))
            load_residual(Step(0, STEPS - 2))
            store(Step(0, STEPS - 3))
            load_residual(Step(0, STEPS - 1))
            store(Step(0, STEPS - 2))
            store(Step(0, STEPS - 1))
            for pr in range(PAIRS):
                sp.wait_ge(stored[pr], 16 * STEPS)

        @block.gpsimd
        def _(pool):
            pool.iota(part_i[:, 0:1], pattern=[[0, 1]], base=0, channel_multiplier=1).then_inc(iotas, 1)
            pool.iota(col_i[:, :], pattern=[[1, P]], base=0, channel_multiplier=0).then_inc(iotas, 1)
            pool.memset(early[:, :], 0.0).then_inc(zeroed, 1)
            pool.memset(minus_half[:, :], -0.5).then_inc(half_ready, 1)
            pool.wait_ge(half_ready, 1)

            def root(at, mv, var_done, rs, sh, rs_done):
                pool.wait_ge(var_done, at.after(4, 3))
                pool.tensor_tensor(rs[:, :], mv[:, :, 1], minus_half[:, :], ALU.pow).then_inc(rs_done, 1)
                pool.wait_ge(rs_done, at.after(2, 0))
                pool.tensor_tensor(sh[:, :], mv[:, :, 0], rs[:, :], ALU.mult).then_inc(rs_done, 1)

            def rest_of_q(at, pr):
                pool.wait_ge(q_out, at.after(2, pr))
                if pr == 0:
                    pool.wait_ge(q_diag_ready, at.before(2))
                pool.tensor_tensor(q_parts[:, 1, pr, :], q32[:, :], q_parts[:, 0, pr, :],
                                   ALU.subtract).then_inc(q_rest, 1)

            def rest_of_k(at, pr):
                pool.wait_ge(k_out, at.after(2, pr))
                real = slice(LEFT, LEFT + T)
                pool.tensor_tensor(k_parts[at.par][:, 1, pr, real], k32[:, :],
                                   k_parts[at.par][:, 0, pr, real], ALU.subtract).then_inc(k_rest, 1)

            def rest_of_v(at, part):
                pool.wait_ge(v_main, at.after(2, part))
                pool.tensor_tensor(half_of_blocks(v_parts[:, 1, :], part), half_of_blocks(vt32[:, :], part),
                                   half_of_blocks(v_parts[:, 0, :], part), ALU.subtract).then_inc(v_rest, 1)

            def sum_rows(at, o):
                pool.wait_ge(exped, at.after(8, 2 * o + 1))
                src = probs[:, o, :, :, :].rearrange("p u b w -> p (u b) w")
                for level in range(LEVELS):
                    width = KB >> (level + 1)
                    if level:
                        pool.wait_ge(summing, at.after(NO * LEVELS, LEVELS * o + level - 1))
                    dst = tree[:, :, 0:width]
                    if level == LEVELS - 1:
                        if at.k > 0 or o >= 2:
                            pool.wait_ge(inverted, at.before(NO) + o - 1)
                        dst = row_sum[:, o % 2, :].unsqueeze(2)
                    pool.tensor_tensor(dst, src[:, :, 0:width], src[:, :, width:2 * width],
                                       ALU.add).then_inc(summing, 1)
                    src = tree

            def normalise(at, o):
                pool.wait_ge(inverted, at.after(NO, o))
                src = probs[:, o, :, :, :].rearrange("p u b w -> p (u b) w")
                pool.tensor_tensor(src, src, inv_sum[:, o % 2, :].unsqueeze(2).broadcast_to([P, CELLS, KB]),
                                   ALU.mult).then_inc(normed, 1)

            def step(at, done2, done, cur, nxt):
                for s in range(SLOTS):
                    if nxt and s == 2:
                        root(at.shift(1), mean_var, x_var, rstd, shift, x_rstd)
                    for st, o in lagged_octet(s, SUM_LAG, cur, done, at):
                        sum_rows(st, o)
                    for st, o in lagged_octet(s, NORM_LAG, cur, done, at):
                        normalise(st, o)
                    if done and s == 7:
                        root(at.shift(-1), mean_var2, x1_var, rstd2, shift2, x1_rstd)
                    if cur and s in (0, 2):
                        rest_of_v(at, s // 2)
                    if nxt and s in (3, 4):
                        rest_of_q(at.shift(1), s - 3)
                    if nxt and s in (4, 5):
                        rest_of_k(at.shift(1), s - 4)

            root(Step(0, 0), mean_var, x_var, rstd, shift, x_rstd)
            for pr in range(PAIRS):
                rest_of_q(Step(0, 0), pr)
                rest_of_k(Step(0, 0), pr)
            run_steps(pool, step)

        @block.scalar
        def _(act):
            def normed_rows(pr, src, dst, rs, sh, ready):
                act.activation(dst[:, pr, :], src[:, pr, :], ACT.Identity, scale=rs[:, pr:pr + 1],
                               bias=sh[:, pr:pr + 1]).then_inc(ready, 1)

            def norm_x(at):
                act.wait_ge(x_rstd, at.after(2, 1))
                act.wait_ge(q_done, at.before(2))
                for pr in range(PAIRS):
                    normed_rows(pr, x_sb, xn, rstd, shift, xn_ready)

            def norm_x1(at, pr):
                act.wait_ge(x1_rstd, at.after(2, 1))
                normed_rows(pr, x1, x2, rstd2, shift2, x2_ready)

            def lay_out(tile, n, rows, b):
                return act.activation(tile[rows, b * C:(b + 1) * C], w_rows[rows, n, :], ACT.Copy)

            act.wait_ge(weights_in, 16 * 5)
            act.wait_ge(zeroed, 1)
            for n, tile in enumerate((wq_in, wk_in)):
                for b in range(2):
                    op = lay_out(tile, n, slice(b * C, (b + 1) * C), b)
                op.then_inc(laid, 1)
            for half in range(2):
                for b in range(2):
                    op = lay_out(wv_in, 2, slice(half * 64 + b * 32, half * 64 + b * 32 + 32), b)
            op.then_inc(laid, 1)
            for n, tile in enumerate((wq_t, wk_t, wv_t)):
                act.wait_ge(w_turned, n + 1)
                act.activation(tile[:, :], ps_s[n][:, 0:P], ACT.Copy).then_inc(wt_copied, 1)
            norm_x(Step(0, 0))
            for b in range(2):
                rows = slice(b * C, (b + 1) * C)
                for pr in range(PAIRS):
                    cols = wo_in[rows, 2 * pr:2 * pr + 2, :].rearrange("p f (h b c) -> p f h b c", b=NB, c=HD)
                    op = act.activation(cols[:, :, :, 2 * pr + b, :],
                                        w_rows[rows, 3, :].rearrange("p (f h c) -> p f h c", f=2, c=HD),
                                        ACT.Copy)
            op.then_inc(laid, 1)
            act.wait_ge(biases_in, 16 * 5)

            def q_taken_out(at, pr):
                act.wait_ge(q_done, at.after(2, pr))
                if not (at.k == 0 and pr == 0):
                    act.wait_ge(q_rest, at.before(2) + pr)
                if at.k > 0 and pr == 0:
                    act.wait_ge(q_diag_ready, at.before(2))
                act.activation(q32[:, :], ps_m[0][:, :], ACT.Identity, bias=bq_sb[:, 0:1])
                act.activation(q_parts[:, 0, pr, :], ps_m[0][:, :], ACT.Identity,
                               bias=bq_sb[:, 0:1]).then_inc(q_out, 1)

            def k_taken_out(at, pr):
                act.wait_ge(k_done, at.after(2, pr))
                if not (at.k == 0 and pr == 0):
                    act.wait_ge(k_rest, at.before(2) + pr)
                act.activation(k32[:, :], ps_m[1][:, :], ACT.Identity, bias=bk_sb[:, 0:1])
                act.activation(k_parts[at.par][:, 0, pr, LEFT:LEFT + T], ps_m[1][:, :], ACT.Identity,
                               bias=bk_sb[:, 0:1]).then_inc(k_out, 1)

            def v_half_out(at, half):
                act.wait_ge(v_done, at.after(2, half))
                act.wait_ge(vt_ready, at.before(2))
                act.activation(v32[:, half, LEFT:LEFT + T], ps_m[half][:, :], ACT.Identity,
                               bias=bv_sb[:, half:half + 1]).then_inc(v_out, 1)

            def main_of_v(at, part):
                if part == 0:
                    act.wait_ge(vt_ready, at.after(2, 1))
                if at.k > 0:
                    act.wait_ge(v_diag_ready, at.shift(-1).after(2, part))
                act.activation(half_of_blocks(v_parts[:, 0, :], part), half_of_blocks(vt32[:, :], part),
                               ACT.Copy).then_inc(v_main, 1)

            def exp_bank(at, k):
                act.wait_ge(shifted, at.after(8, k))
                if at.k > 0:
                    act.wait_ge(turned, at.shift(-1).after(8, 2 * (k // 2) + 1))
                act.activation(bank_of_probs(k),
                               ps_s[k % S_BANKS][:, :].rearrange("p (u q w) -> p u q w", q=PAIRS, w=KB),
                               ACT.Exp, scale=float(HD) ** -0.5).then_inc(exped, 1)

            def window_bank(at, k):
                act.wait_ge(exped, at.after(8, k))
                act.activation(ps_s[k % S_BANKS][:, :].rearrange("p (c w) -> p c w", w=KB),
                               window[:, :].unsqueeze(1).broadcast_to([P, 16, KB]),
                               ACT.Copy).then_inc(windowed, 1)

            def main_of_probs(at, q):
                act.wait_ge(turned, at.after(8, q))
                if at.k > 0 or q >= 2:
                    act.wait_ge(valued, at.before(8) + q - 1)
                act.activation(pt[:, q % 2, 0, :, :],
                               ps_t[q % 2][:, :].rearrange("p (u c) -> p u c", c=P), ACT.Copy).then_inc(p_main, 1)

            def take_out(at, q):
                act.wait_ge(valued, at.after(8, q))
                if q == 0 and at.k > 1:
                    act.wait_ge(wo_done, at.shift(-1).before(2))
                for h in range(HH):
                    op = act.activation(*of_head(at, q, h), ACT.Copy)
                op.then_inc(att_ready, 1)

            def main_of_x2(at, pr):
                act.wait_ge(x2_ready, at.after(2, pr))
                if at.k > 0:
                    act.wait_ge(ft_done, at.shift(-1).after(2, pr))
                act.activation(x2_parts[:, pr, 0, :], x2[:, pr, :], ACT.Copy).then_inc(x2_main, 1)

            def x2_turned_out(at, pr):
                act.wait_ge(ft_done, at.after(2, pr))
                if at.k > 0:
                    act.wait_ge(ff_done, at.shift(-1).after(2, pr))
                act.activation(x2t[:, pr, :], ps_m[pr][:, :].bitcast(F16), ACT.Copy).then_inc(ft_out, 1)

            def ffn_out(at, pr):
                act.wait_ge(ff_done, at.after(2, pr))
                if at.k > 0:
                    act.wait_ge(out_ready, at.shift(-1).after(2, pr))
                act.activation(ff16[:, pr, :], ps_m[pr][:, :], ACT.Copy).then_inc(ff_out, 1)

            def step(at, done2, done, cur, nxt):
                for s in range(SLOTS):
                    if done2 and s == 1:
                        x2_turned_out(at.shift(-2), 0)
                        x2_turned_out(at.shift(-2), 1)
                    if done2 and s in (2, 3):
                        ffn_out(at.shift(-2), s - 2)
                    if nxt and s == 2:
                        norm_x(at.shift(1))
                    if cur and s in (0, 2):
                        main_of_v(at, s // 2)
                    if nxt and s in (3, 4):
                        q_taken_out(at.shift(1), s - 3)
                    if nxt and s in (4, 5):
                        k_taken_out(at.shift(1), s - 4)
                    if nxt and s in (5, 6):
                        v_half_out(at.shift(1), s - 5)
                    if cur:
                        exp_bank(at, s)
                    for st, q in lagged(s, VALUE_LAG, cur, done, at):
                        take_out(st, q)
                    for st, q in lagged(s, TURN_LAG, cur, done, at):
                        main_of_probs(st, q)
                    if cur:
                        window_bank(at, s)
                    if done and s == 7:
                        norm_x1(at.shift(-1), 0)
                        norm_x1(at.shift(-1), 1)
                        main_of_x2(at.shift(-1), 0)
                        main_of_x2(at.shift(-1), 1)

            for pr in range(PAIRS):
                q_taken_out(Step(0, 0), pr)
                k_taken_out(Step(0, 0), pr)
            v_half_out(Step(0, 0), 0)
            v_half_out(Step(0, 0), 1)
            act.wait_ge(w_turned, 4)
            act.activation(wo_t[:, :, :], ps_t[1][:, :].rearrange("p (n c) -> p n c", c=P),
                           ACT.Copy).then_inc(wt_copied, 1)
            run_steps(act, step)

        @block.vector
        def _(dve):
            counts = {}

            def in_order(signal, *instructions):
                for instruction in instructions:
                    counts[signal.name] = counts.get(signal.name, 0) + 1
                    instruction.then_inc(signal, 1)
                dve.wait_ge(signal, counts[signal.name])

            def statistics(pr, src, st, stats_done):
                dve.bn_stats(st[:, pr, :], src[:, pr, :]).then_inc(stats_done, 1)

            def aggregate(at, st, stats_done, mv, var_done):
                dve.wait_ge(stats_done, at.after(2, 1))
                dve.memset(gate[:, :], 0.0)
                for pr in range(PAIRS):
                    dve.bn_aggr(mv[:, pr, :], st[:, pr, :]).then_inc(var_done, 1)
                dve.wait_ge(var_done, at.after(4, 1))
                dve.tensor_scalar(mv[:, :, 0], mv[:, :, 0], -1.0, None, ALU.mult).then_inc(var_done, 1)
                dve.tensor_scalar(mv[:, :, 1], mv[:, :, 1], EPS, None, ALU.add).then_inc(var_done, 1)

            def moments_x(at):
                dve.wait_ge(x_in, at.before(16) + 16)
                for pr in range(PAIRS):
                    statistics(pr, x_sb, stats, x_stats)
                aggregate(at, stats, x_stats, mean_var, x_var)

            def q_diagonals(at, pr):
                dve.wait_ge(q_rest, at.after(2, pr))
                if at.k >= 2 and pr == 0:
                    dve.wait_ge(scored, at.shift(-1).before(8))
                src = q_parts[:, :, pr, :].rearrange("p a (u t) -> p a u t", t=QB)
                dst = q_diag[at.par][:, :, :, :].rearrange("p (a q u) h t -> p a q u h t", a=2, q=PAIRS)
                for h in range(H):
                    op = dve.tensor_scalar(dst[:, :, pr, :, h, :], src, head_of_row[:, h:h + 1], None, ALU.mult)
                op.then_inc(q_diag_ready, 1)

            def turn_v(at, half):
                dve.wait_ge(v_out, at.after(2, half))
                if half == 0:
                    dve.wait_ge(v_rest, at.before(2))
                keys = v32[:, half, :]
                src = bass.AP(keys.tensor, keys.offset, [keys.ap[0], [QB, NU], [1, KB]])
                dst = vt32[:, half * NU * KB:(half + 1) * NU * KB].rearrange("p (u c) -> p u c", c=KB)
                dve.transpose(dst, src).then_inc(vt_ready, 1)

            def v_diagonals(at, part, batches):
                if batches[0] == 0:
                    dve.wait_ge(v_rest, at.after(2, part))
                    dve.wait_ge(valued, at.before(8) - (4 if part == 0 and at.k else 0))
                blocks = slice(part * NU // 2, (part + 1) * NU // 2)
                src = v_parts[:, :, :].rearrange("p a (f u h c) -> p (a f) u h c", f=2, h=HH, c=HD)[:, :, blocks]
                for b in batches:
                    op = dve.tensor_scalar(v_diag[:, :, blocks, :, b, :], src, batch_of_row[:, b:b + 1], None, ALU.mult)
                if batches[-1] == NB - 1:
                    op.then_inc(v_diag_ready, 1)

            def maxima(at, k):
                dve.wait_ge(scored, at.after(8, k))
                dve.tensor_reduce(row_max[:, k % S_BANKS, :],
                                  ps_s[k % S_BANKS][:, :].rearrange("p (c w) -> p c w", w=KB),
                                  AX.X, ALU.max).then_inc(maxed, 1)

            def invert(at, o):
                dve.wait_ge(summing, at.after(NO * LEVELS, LEVELS * o + LEVELS - 1))
                if at.k > 0 or o >= 2:
                    dve.wait_ge(normed, at.before(NO) + o - 1)
                dve.reciprocal(inv_sum[:, o % 2, :], row_sum[:, o % 2, :]).then_inc(inverted, 1)

            def rest_of_probs(at, q):
                dve.wait_ge(p_main, at.after(8, q))
                dve.tensor_tensor(pt[:, q % 2, 1, :, :], ps_t[q % 2][:, :].rearrange("p (u c) -> p u c", c=P),
                                  pt[:, q % 2, 0, :, :], ALU.subtract).then_inc(p_rest, 1)

            def residual(at, pr):
                if pr == 0:
                    dve.wait_ge(xr_in, at.before(16) + 16)
                dve.wait_ge(wo_done, at.after(2, pr))
                dve.wait_ge(stored[pr], at.before(16))
                dve.scalar_tensor_tensor(x1[:, pr, :], ps_m[pr][:, :], bo_sb[:, 0:1], xr_sb[:, pr, :],
                                         ALU.add, ALU.add).then_inc(x1_ready, 1)

            def moments_x1(at, pr):
                dve.wait_ge(x1_ready, at.after(2, pr))
                statistics(pr, x1, stats2, x1_stats)
                if pr == PAIRS - 1:
                    aggregate(at, stats2, x1_stats, mean_var2, x1_var)

            def rest_of_x2(at, pr):
                dve.wait_ge(x2_main, at.after(2, pr))
                dve.wait_ge(x2_ready, at.after(2, pr))
                dve.tensor_tensor(x2_parts[:, pr, 1, :], x2[:, pr, :], x2_parts[:, pr, 0, :],
                                  ALU.subtract).then_inc(x2_rest, 1)

            def outputs(at, pr):
                dve.wait_ge(ff_out, at.after(2, pr))
                dve.tensor_tensor(ff16[:, pr, :], ff16[:, pr, :], bias_sb[:, :], ALU.add).then_inc(ff_biased, 1)
                dve.wait_ge(ff_biased, at.after(2, pr))
                dve.tensor_tensor(x1[:, pr, :], x1[:, pr, :], ff16[:, pr, :], ALU.add).then_inc(out_ready, 1)

            def group_tables():
                dve.wait_ge(ffn_in, 16 * N_FFN_LOADS)
                zi = z_i[0:GROUPS, :].rearrange("g (w j) -> g w j", j=NIB)
                g, neg = g_f[0:GROUPS, :], gneg_f[0:GROUPS, :]
                in_order(tables, *(dve.tensor_scalar(zi[:, :, j], z_in[0:GROUPS, :], 4 * j, 15,
                                                     ALU.logical_shift_right, ALU.bitwise_and)
                                   for j in range(NIB)),
                         dve.tensor_copy(g, g_i[0:GROUPS, :]))
                in_order(tables, dve.tensor_copy(z_h[0:GROUPS, :], z_i[0:GROUPS, :]),
                         dve.tensor_scalar(neg, g, 0.0, float(GROUPS), ALU.is_lt, ALU.mult))
                in_order(tables, dve.tensor_tensor(g, g, neg, ALU.add))
                in_order(tables, dve.tensor_scalar(g, g, 0.0, float(GROUPS - 1), ALU.max, ALU.min))
                in_order(tables_ready, dve.tensor_scalar(hot_h[0:GROUPS, :], g, part_f[0:GROUPS, 0:1], None,
                                                         ALU.is_equal))

            def dequantise(c):
                if c == 0:
                    dve.wait_ge(words_in, 16 * KC)
                in_order(dequant, dve.tensor_tensor(words[c], words[c],
                                                    shift_i[:, 0:1].broadcast_to([P, OUT_F]),
                                                    ALU.logical_shift_right))
                in_order(dequant, dve.tensor_scalar(words[c], words[c], 15, None, ALU.bitwise_and))
                dve.wait_ge(spread, 2 * c + 1)
                in_order(dequant, dve.tensor_tensor(lev_h, words[c], ps_t[1][:, :], ALU.subtract))
                dve.wait_ge(spread, 2 * c + 2)
                in_order(dequant, dve.tensor_tensor(w_ffn[:, c, :], lev_h, ps_o[:, :], ALU.mult))

            def step(at, done2, done, cur, nxt):
                for s in range(SLOTS):
                    if cur:
                        maxima(at, s)
                    for st, q in lagged(s, REST_LAG, cur, done, at):
                        rest_of_probs(st, q)
                    if cur and not done and s == 0:
                        group_tables()
                    if cur and not done and 1 <= s <= KC:
                        dequantise(s - 1)
                    if done2 and s == 0:
                        rest_of_x2(at.shift(-2), 0)
                        rest_of_x2(at.shift(-2), 1)
                    if nxt and s == 1:
                        moments_x(at.shift(1))
                    if done and s == 1:
                        v_diagonals(at.shift(-1), 1, range(2, NB))
                    if cur and s in (2, 3):
                        v_diagonals(at, 0, (range(0, 2), range(2, NB))[s - 2])
                    if done2 and s in (2, 3):
                        outputs(at.shift(-2), s - 2)
                    if nxt and s in (4, 5):
                        q_diagonals(at.shift(1), s - 4)
                    if nxt and s == 6:
                        turn_v(at.shift(1), 0)
                    if done and s in (6, 7):
                        residual(at.shift(-1), s - 6)
                        moments_x1(at.shift(-1), s - 6)
                    if cur and s in (5, 6):
                        v_diagonals(at, 1, range(s - 5, s - 4))
                    if nxt and s == 7:
                        turn_v(at.shift(1), 1)
                    for st, o in lagged_octet(s, SUM_LAG, cur, done, at):
                        invert(st, o)

            first = Step(0, 0)
            dve.wait_ge(iotas, 2)
            in_order(consts, dve.tensor_scalar(part_i[:, 1:2], part_i[:, 0:1], QB - 1, None, ALU.bitwise_and),
                     dve.tensor_scalar(part_i[:, 2:3], part_i[:, 0:1], 3, H - 1, ALU.logical_shift_right,
                                       ALU.bitwise_and),
                     dve.tensor_scalar(part_i[:, 3:4], part_i[:, 0:1], 5, None, ALU.logical_shift_right),
                     dve.tensor_copy(col_f[:, :], col_i[:, :]))
            in_order(consts, dve.tensor_copy(part_f[:, :], part_i[:, :]))
            in_order(ident_ready, dve.tensor_scalar(ident[:, :], col_f[:, :], part_f[:, 0:1], None,
                                                    ALU.is_equal))
            moments_x(first)
            in_order(consts,
                     dve.tensor_scalar(head_of_row[:, :], col_f[:, 0:H], part_f[:, 2:3], None, ALU.is_equal),
                     dve.tensor_scalar(batch_of_row[:, :], col_f[:, 0:NB], part_f[:, 3:4], None, ALU.is_equal),
                     dve.tensor_scalar(minus_ident[:, :], ident[:, :], -1.0, None, ALU.mult),
                     dve.tensor_copy(ident16[:, :], ident[:, :]),
                     dve.tensor_scalar(shift_i[:, :], part_i[:, 0:1], 7, 2, ALU.bitwise_and,
                                       ALU.logical_shift_left))
            in_order(consts, dve.tensor_scalar(ahead, col_f[:, 0:KB], part_f[:, 1:2], None, ALU.subtract))
            in_order(consts, dve.tensor_scalar(before, ahead, 0.0, MASKED, ALU.is_lt, ALU.mult),
                     dve.tensor_scalar(beyond, ahead, float(WIN - 1), MASKED, ALU.is_gt, ALU.mult))
            for edge in (slice(0, LEFT), slice(LEFT + T, TP)):
                in_order(consts, *(dve.memset(k_parts[par][:, :, :, edge], 0.0) for par in range(2)),
                         dve.memset(v32[:, :, edge], 0.0))
            in_order(consts_ready, dve.tensor_tensor(window[:, :], before, beyond, ALU.add))

            dve.wait_ge(biases_in, 16 * 5)
            q_diagonals(first, 0)
            q_diagonals(first, 1)
            turn_v(first, 0)
            turn_v(first, 1)
            run_steps(dve, step)

        @block.tensor
        def _(pe):
            def turn_weight(bank, n, tile):
                return pe.transpose(bank[:, n * P:(n + 1) * P], tile, ident[:, :])

            pe.wait_ge(ident_ready, 1)
            for n, tile in enumerate((wq_in, wk_in, wv_in)):
                pe.wait_ge(laid, n + 1)
                turn_weight(ps_s[n], 0, tile).then_inc(w_turned, 1)

            def spread_groups(c):
                hot = hot_h[0:GROUPS, c * P:(c + 1) * P]
                if c == 0:
                    pe.wait_ge(tables_ready, 1)
                    pe.wait_ge(wt_copied, 4)
                else:
                    pe.wait_ge(dequant, 4 * c - 1)
                pe.matmul(ps_t[1][:, :], hot, z_h[0:GROUPS, :], start=True, stop=True).then_inc(spread, 1)
                if c > 0:
                    pe.wait_ge(dequant, 4 * c)
                pe.matmul(ps_o[:, :], hot, s_h[0:GROUPS, :], start=True, stop=True).then_inc(spread, 1)

            def bank_free(at, pr):
                if at.k > 0:
                    pe.wait_ge(v_out, at.shift(-1).after(2, pr))
                if at.k > 2:
                    pe.wait_ge(ff_out, at.shift(-3).after(2, pr))

            def project_q(at, pr):
                pe.wait_ge(xn_ready, at.after(2, pr))
                if pr == 0:
                    bank_free(at, 0)
                else:
                    pe.wait_ge(q_out, at.after(2, 0))
                pe.matmul(ps_m[0][:, :], wq_t[:, :], xn[:, pr, :], start=True, stop=True).then_inc(q_done, 1)

            def project_k(at, pr):
                if pr == 0:
                    pe.wait_ge(c_in, at.before(16) + 16)
                    bank_free(at, 1)
                else:
                    pe.wait_ge(k_out, at.after(2, 0))
                pe.matmul(ps_m[1][:, :], wk_t[:, :], c_sb[:, pr, :], start=True, stop=True).then_inc(k_done, 1)

            def project_v(at, half):
                pe.wait_ge(k_out if half else q_out, at.after(2, 1))
                for pr in range(PAIRS):
                    last = pe.matmul(ps_m[half][pr * 64:pr * 64 + 64, :], wv_t[:, half * 64:half * 64 + 64],
                                     c_sb[:, pr, :], start=True, stop=True)
                last.then_inc(v_done, 1)

            def scores(at, k):
                octet, side = k // 2, k % 2
                bank = ps_s[k % S_BANKS]
                if k == 0:
                    pe.wait_ge(q_diag_ready, at.after(2, 1))
                    pe.wait_ge(k_rest, at.after(2, 1))
                if k >= S_BANKS:
                    pe.wait_ge(windowed, at.after(8, k - S_BANKS))
                elif at.k > 0:
                    pe.wait_ge(windowed, at.shift(-1).after(8, LAST_ON_BANK[k]))
                rows = slice(side * 64, side * 64 + 64)
                for u in range(OCT):
                    for pr in range(PAIRS):
                        blk = octet * OCT + u
                        cell = (u * PAIRS + pr) * KB
                        for qp, kp in ((0, 0), (0, 1), (1, 0)):
                            last = pe.matmul(bank[:, cell:cell + KB],
                                             q_diag[at.par][rows, (qp * PAIRS + pr) * NU + blk, :, :]
                                             .rearrange("p h t -> p (h t)"),
                                             k_parts[at.par][rows, kp, pr, blk * QB:blk * QB + KB],
                                             start=False, stop=False, skip_group_check=True)
                last.then_inc(scored, 1)

            def shift_scores(at, k):
                pe.wait_ge(maxed, at.after(8, k))
                pe.matmul(ps_s[k % S_BANKS][:, :].rearrange("p (c w) -> p c w", w=KB), minus_ident[:, :],
                          row_max[:, k % S_BANKS, :].unsqueeze(2).broadcast_to([P, 16, KB]),
                          start=False, stop=True, skip_group_check=True).then_inc(shifted, 1)

            def turn_probs(at, q):
                pe.wait_ge(normed, at.after(NO, q // 2))
                if at.k > 0 or q >= 2:
                    pe.wait_ge(p_rest, at.before(8) + q - 1)
                elif q == 1:
                    pe.wait_ge(dequant, 4 * KC)
                for j in range(4):
                    last = pe.transpose(ps_t[q % 2][:, j * P:(j + 1) * P],
                                        probs[:, q // 2, 4 * (q % 2) + j, :, :].rearrange("p b w -> p (b w)"),
                                        ident[:, :])
                last.then_inc(turned, 1)

            def values(at, q):
                if q in (0, NQ // 2):
                    pe.wait_ge(v_diag_ready, at.after(2, q // (NQ // 2)))
                pe.wait_ge(p_rest, at.after(8, q))
                if at.k > 0 or q > 0:
                    pe.wait_ge(att_ready, at.before(8) + q)
                for half in range(2):
                    for j in range(4):
                        cell = (half * 4 + j) * 64
                        terms = ((0, 0), (0, 1), (1, 0))
                        for n, (vp, pp) in enumerate(terms):
                            last = pe.matmul(ps_o[:, cell:cell + 64],
                                             v_diag[:, vp * 2 + half, 4 * q + j, :, :, :]
                                             .rearrange("p h b c -> p (h b c)"),
                                             pt[:, q % 2, pp, j, half * 64:half * 64 + 64],
                                             start=n == 0, stop=n == len(terms) - 1)
                last.then_inc(valued, 1)

            def project_out(at, pr, nxt, quads=range(NQ)):
                pe.wait_ge(att_ready, at.after(8, quads[-1]))
                if nxt:
                    pe.wait_ge(v_out, at.shift(2).after(2, pr))
                else:
                    pe.wait_ge(ff_out, at.shift(-1).after(2, pr))
                some = slice(quads[0], quads[-1] + 1)
                for half in range(2):
                    last = pe.matmul(ps_m[pr][:, quads[0] * 64:(quads[-1] + 1) * 64], wo_t[:, 2 * pr + half, :],
                                     att[at.par][:, some, half, :], start=half == 0, stop=half == 1)
                if quads[-1] == NQ - 1:
                    last.then_inc(wo_done, 1)

            def turn_x2(at, pr):
                pe.wait_ge(x2_rest, at.after(2, pr))
                for part in range(2):
                    for c in range(KC):
                        n = part * KC + c
                        last = pe.transpose(ps_m[pr][:, :].bitcast(F16)[:, n * P:(n + 1) * P],
                                            x2_parts[:, pr, part, c * P:(c + 1) * P], ident16[:, :])
                last.then_inc(ft_done, 1)

            def feed_forward(at, pr):
                pe.wait_ge(ft_out, at.after(2, pr))
                for n in range(2 * KC):
                    last = pe.matmul(ps_m[pr][:, :], x2t[:, pr, n * P:(n + 1) * P], w_ffn[:, n % KC, :],
                                     start=n == 0, stop=n == 2 * KC - 1)
                last.then_inc(ff_done, 1)

            def step(at, done2, done, cur, nxt):
                for s in range(SLOTS):
                    if cur and not done and 1 <= s <= KC:
                        spread_groups(s - 1)
                    for st, q in lagged(s, VALUE_LAG, cur, done, at):
                        values(st, q)
                    if cur:
                        shift_scores(at, s)
                    for st, q in lagged(s, TURN_LAG, cur, done, at):
                        turn_probs(st, q)
                    if cur and s < SLOTS - 1:
                        scores(at, s + 1)
                    if done2 and s == 0:
                        turn_x2(at.shift(-2), 0)
                        turn_x2(at.shift(-2), 1)
                    if nxt and s == SLOTS - 1:
                        scores(at.shift(1), 0)
                    if done2 and s in (1, 2):
                        feed_forward(at.shift(-2), s - 1)
                    if nxt and s in (2, 3):
                        project_q(at.shift(1), s - 2)
                    if nxt and s in (3, 4):
                        project_k(at.shift(1), s - 3)
                    if nxt and s in (4, 5):
                        project_v(at.shift(1), s - 4)
                    if done and (nxt or cur) and s in (5, 6):
                        project_out(at.shift(-1), s - 5, nxt)
                    if done and not cur and s in (4, 6):
                        for pr in range(PAIRS):
                            project_out(at.shift(-1), pr, nxt, (range(0, 6), range(6, NQ))[s // 6])

            first = Step(0, 0)
            pe.wait_ge(wt_copied, 3)
            for pr in range(PAIRS):
                project_q(first, pr)
                project_k(first, pr)
            pe.wait_ge(consts_ready, 1)
            for bank in ps_s:
                pe.matmul(bank[:, :].rearrange("p (c w) -> p c w", w=KB), ident[:, :],
                          window[:, :].unsqueeze(1).broadcast_to([P, 16, KB]),
                          start=True, stop=False, skip_group_check=True)
            project_v(first, 0)
            project_v(first, 1)
            pe.wait_ge(laid, 4)
            for n in range(4):
                last = turn_weight(ps_t[1], n, wo_in[:, n, :])
            last.then_inc(w_turned, 1)
            scores(first, 0)
            run_steps(pe, step)


_INS = ['x', 'ctx_4096', 'L0_xattn_Wq', 'L0_xattn_bq', 'L0_xattn_Wk', 'L0_xattn_bk', 'L0_xattn_Wv', 'L0_xattn_bv',
        'L0_xattn_Wo', 'L0_xattn_bo', 'L0_ffn_qweight', 'L0_ffn_qzeros', 'L0_ffn_scales', 'L0_ffn_g_idx',
        'L0_ffn_bias']


def kernel(**inputs):
    import numpy as _np
    import concourse.bacc as _bacc
    from concourse import mybir as _mybir
    from concourse.bass_utils import run_bass_kernel_spmd as _run

    nc = _bacc.Bacc("TRN2", target_bir_lowering=False, num_devices=1)
    arrays, args = {}, []
    for name in _INS:
        a = _np.ascontiguousarray(inputs[name])
        arrays[f"in_{name}"] = a
        args.append(nc.dram_tensor(f"in_{name}", a.shape, _mybir.dt.from_np(a.dtype), kind="ExternalInput").ap())
    result = nc.dram_tensor("result", (B, C, T), F32, kind="ExternalOutput").ap()
    build(nc, *args, result)
    r = _run(nc, [arrays], core_ids=[0])
    return r.results[0]["result"]
```
